# Optimizing a Trainium2 kernel written in Bass

```python
import numpy as np
import jax
import jax.numpy as jnp

def _softmax(x, axis=-1):
    return jax.nn.softmax(x, axis=axis)

def _gelu(x):
    return jax.nn.gelu(x, approximate=True)

def _silu(x):
    return jax.nn.silu(x)

def _sigmoid(x):
    return jax.nn.sigmoid(x)

def _layernorm(x, axis=-1, eps=1e-05):
    m = jnp.mean(x, axis=axis, keepdims=True)
    v = jnp.var(x, axis=axis, keepdims=True)
    return (x - m) / jnp.sqrt(v + eps)

def _scatter_add(tgt, idx, src, axis=0):
    return tgt.at[idx].add(src)

def _segment_sum(src, seg, n):
    return jax.ops.segment_sum(src, seg, n)
kernel_name = 'mk_adj_resnorm_d4_adj_r2_82d9f9'

def setup_inputs(seed: int=0):
    np.random.seed(seed)
    _w = jnp.asarray

    def _rec_inputs():
        import jax
        import jax.numpy as jnp
        _gk = jax.random.key(seed)
        x = -9.806e-05 + 1 * jax.random.normal(jax.random.fold_in(_gk, 1), (4096, 64), jnp.float32)
        _w = (1.0 + jnp.arange(4096, dtype=jnp.float32)) ** (-0.5)
        _w = _w / _w.mean()
        _pij = jnp.clip(0.000488281 * _w[:, None] * _w[None, :], 0.0, 1.0)
        _a = jax.random.uniform(jax.random.fold_in(_gk, 2), (4096, 4096)) < _pij
        _af = _a.astype(jnp.float32)
        adj = _af
        return (x, adj)
    x, adj = _rec_inputs()

    def _L0_gnn_setup():
        import jax, jax.numpy as jnp
        import numpy as np
        N, D_IN, D_OUT = (4096, 64, 64)
        MAX_NEIGH = 100
        DECAY = 0.5
        key = jax.random.key(seed)
        k1, k2, k3, k4 = jax.random.split(key, 4)
        stdv = 1.0 / np.sqrt(D_OUT)
        inputs = {'input': jax.random.normal(k1, (N, D_IN), dtype=jnp.float32), 'adj': jax.random.randint(k2, (N, N), 0, 2).astype(jnp.float32), 'weight': jax.random.uniform(k3, (D_IN, D_OUT), minval=-stdv, maxval=stdv, dtype=jnp.float32), 'bias': jax.random.uniform(k4, (D_OUT,), minval=-stdv, maxval=stdv, dtype=jnp.float32)}
        return inputs
    _L0_gnn_all = _L0_gnn_setup()
    _L0_gnn_in = {k: v for k, v in _L0_gnn_all.items() if k in ('weight', 'bias')}
    del _L0_gnn_all

    def _L1_gnn_setup():
        import jax, jax.numpy as jnp
        import numpy as np
        N, D = (6144, 64)

        def _ggc(x, adj, W, wih, whh, bih, bhh):
            m = adj @ (x @ W)
            gi = m @ wih.T + bih
            gh = x @ whh.T + bhh
            i_r, i_z, i_n = jnp.split(gi, 3, axis=-1)
            h_r, h_z, h_n = jnp.split(gh, 3, axis=-1)
            r = jax.nn.sigmoid(i_r + h_r)
            z = jax.nn.sigmoid(i_z + h_z)
            n = jnp.tanh(i_n + r * h_n)
            return (1.0 - z) * n + z * x
        key = jax.random.key(seed)
        ks = jax.random.split(key, 8)
        s = 1.0 / np.sqrt(D)
        return {'x': jax.random.normal(ks[0], (N, D), jnp.float32), 'adj': jax.random.uniform(ks[1], (N, N), jnp.float32), 'W1': jax.random.normal(ks[2], (D, D), jnp.float32) * s, 'wih1': jax.random.normal(ks[3], (3 * D, D), jnp.float32) * s, 'whh1': jax.random.normal(ks[4], (3 * D, D), jnp.float32) * s, 'bih1': jnp.zeros((3 * D,), jnp.float32), 'bhh1': jnp.zeros((3 * D,), jnp.float32), 'W2': jax.random.normal(ks[5], (D, D), jnp.float32) * s, 'wih2': jax.random.normal(ks[6], (3 * D, D), jnp.float32) * s, 'whh2': jax.random.normal(ks[7], (3 * D, D), jnp.float32) * s, 'bih2': jnp.zeros((3 * D,), jnp.float32), 'bhh2': jnp.zeros((3 * D,), jnp.float32)}
    _L1_gnn_all = _L1_gnn_setup()
    _L1_gnn_in = {k: v for k, v in _L1_gnn_all.items() if k in ('W1', 'wih1', 'whh1', 'bih1', 'bhh1', 'W2', 'wih2', 'whh2', 'bih2', 'bhh2')}
    del _L1_gnn_all

    def _L2_gnn_setup():
        import jax, jax.numpy as jnp
        import numpy as np
        N = 8192
        IN_C = 64
        OUT_C = 64
        key = jax.random.key(seed)
        k1, k2, k3 = jax.random.split(key, 3)
        g_data = jax.random.normal(k1, (N, IN_C), dtype=jnp.float32)
        g_adj = jax.random.uniform(k2, (N, N), dtype=jnp.float32)
        bound = 1.44 * np.sqrt(6.0 / (IN_C + OUT_C))
        W = jax.random.uniform(k3, (IN_C, OUT_C), dtype=jnp.float32, minval=-bound, maxval=bound)
        return {'g_data': g_data, 'g_adj': g_adj, 'W': W}
    _L2_gnn_all = _L2_gnn_setup()
    _L2_gnn_in = {k: v for k, v in _L2_gnn_all.items() if k in ('W',)}
    del _L2_gnn_all

    def _L3_gnn_setup():
        import jax, jax.numpy as jnp
        import numpy as np
        N = 8192
        F_IN = 64
        F_OUT = 64
        key = jax.random.key(seed)
        k1, k2, k3 = jax.random.split(key, 3)
        features = jax.random.normal(k1, (N, F_IN), dtype=jnp.float32)
        adj = jax.random.uniform(k2, (N, N), dtype=jnp.float32)
        W = jax.random.normal(k3, (F_OUT, 2 * F_IN), dtype=jnp.float32)
        return {'features': features, 'adj': adj, 'W': W}
    _L3_gnn_all = _L3_gnn_setup()
    _L3_gnn_in = {k: v for k, v in _L3_gnn_all.items() if k in ('W',)}
    del _L3_gnn_all
    return {'x': x, 'adj': adj, 'L0_gnn_weight': _L0_gnn_in['weight'], 'L0_gnn_bias': _L0_gnn_in['bias'], 'L1_gnn_W1': _L1_gnn_in['W1'], 'L1_gnn_wih1': _L1_gnn_in['wih1'], 'L1_gnn_whh1': _L1_gnn_in['whh1'], 'L1_gnn_bih1': _L1_gnn_in['bih1'], 'L1_gnn_bhh1': _L1_gnn_in['bhh1'], 'L1_gnn_W2': _L1_gnn_in['W2'], 'L1_gnn_wih2': _L1_gnn_in['wih2'], 'L1_gnn_whh2': _L1_gnn_in['whh2'], 'L1_gnn_bih2': _L1_gnn_in['bih2'], 'L1_gnn_bhh2': _L1_gnn_in['bhh2'], 'L2_gnn_W': _L2_gnn_in['W'], 'L3_gnn_W': _L3_gnn_in['W']}

def reference(x, adj, L0_gnn_weight, L0_gnn_bias, L1_gnn_W1, L1_gnn_wih1, L1_gnn_whh1, L1_gnn_bih1, L1_gnn_bhh1, L1_gnn_W2, L1_gnn_wih2, L1_gnn_whh2, L1_gnn_bih2, L1_gnn_bhh2, L2_gnn_W, L3_gnn_W):
    import jax
    import jax.numpy as jnp

    def _L0_gnn_ref(input, adj, weight, bias):
        import jax, jax.numpy as jnp
        import numpy as np
        N, D_IN, D_OUT = (4096, 64, 64)
        MAX_NEIGH = 100
        DECAY = 0.5
        support = input @ weight
        mask = (adj != 0).astype(support.dtype)
        rank = jnp.cumsum(mask, axis=1)
        deg = rank[:, -1:]
        k = jnp.minimum(deg, float(MAX_NEIGH))
        pos = rank - (deg - k)
        w = mask * jnp.where(pos > 0, DECAY ** (k - pos), 0.0)
        out = w @ support + bias
        return out

    def _L1_gnn_ref(x, adj, W1, wih1, whh1, bih1, bhh1, W2, wih2, whh2, bih2, bhh2):
        import jax, jax.numpy as jnp
        import numpy as np
        N, D = (6144, 64)

        def _ggc(x, adj, W, wih, whh, bih, bhh):
            m = adj @ (x @ W)
            gi = m @ wih.T + bih
            gh = x @ whh.T + bhh
            i_r, i_z, i_n = jnp.split(gi, 3, axis=-1)
            h_r, h_z, h_n = jnp.split(gh, 3, axis=-1)
            r = jax.nn.sigmoid(i_r + h_r)
            z = jax.nn.sigmoid(i_z + h_z)
            n = jnp.tanh(i_n + r * h_n)
            return (1.0 - z) * n + z * x
        h = jax.nn.relu(_ggc(x, adj, W1, wih1, whh1, bih1, bhh1))
        return jax.nn.relu(_ggc(h, adj, W2, wih2, whh2, bih2, bhh2))

    def _L2_gnn_ref(g_data, g_adj, W):
        import jax, jax.numpy as jnp
        import numpy as np
        N = 8192
        IN_C = 64
        OUT_C = 64
        n = g_adj.shape[0]
        a = g_adj + jnp.eye(n, dtype=g_adj.dtype)
        deg = a.sum(axis=1)
        dinv = jnp.where(deg > 0, deg ** (-0.5), 0.0)
        a_norm = dinv[:, None] * a * dinv[None, :]
        out = a_norm @ g_data
        out = out @ W
        return out

    def _L3_gnn_ref(features, adj, W):
        import jax, jax.numpy as jnp
        import numpy as np
        N = 8192
        F_IN = 64
        F_OUT = 64
        neigh = jnp.matmul(adj, features)
        deg = jnp.sum(adj, axis=1, keepdims=True) + 1.0
        neigh = neigh / deg
        data = jnp.concatenate([features, neigh], axis=-1)
        return jnp.matmul(data, W.T)
    x = _layernorm(x + _L0_gnn_ref(x, adj, L0_gnn_weight, L0_gnn_bias), axis=-1)
    x = _layernorm(x + _L1_gnn_ref(x, adj, L1_gnn_W1, L1_gnn_wih1, L1_gnn_whh1, L1_gnn_bih1, L1_gnn_bhh1, L1_gnn_W2, L1_gnn_wih2, L1_gnn_whh2, L1_gnn_bih2, L1_gnn_bhh2), axis=-1)
    x = _layernorm(x + _L2_gnn_ref(x, adj, L2_gnn_W), axis=-1)
    x = _layernorm(x + _L3_gnn_ref(x, adj, L3_gnn_W), axis=-1)
    return x

_drawn_inputs = setup_inputs


def setup_inputs(seed=0):
    import zlib

    import numpy as np

    out = dict(_drawn_inputs(seed))
    spreads = {'L1_gnn_bih1': (0.0, 0.445),
     'L1_gnn_bhh1': (0.0, 0.8),
     'L1_gnn_bih2': (0.0, 0.1),
     'L1_gnn_bhh2': (0.0, 0.468)}
    factors = {}
    for name, (base, spread) in spreads.items():
        noise = np.random.default_rng([zlib.crc32(name.encode()), seed]).standard_normal(out[name].shape)
        drawn = base * np.exp(spread * noise) if base else spread * noise
        out[name] = jnp.asarray(drawn.astype(out[name].dtype))
    for name, factor in factors.items():
        out[name] = (out[name] * factor).astype(out[name].dtype)
    return out
```

```python
from contextlib import ExitStack

import concourse.bass as bass
from concourse import mybir

N, D = 4096, 64
P = 128
JB = N // P
GC = 512
G = N // GC
B = GC // P
Q = G // 2
JP = JB // 2
NLOAD = 16
MAX_NEIGH = 100
STEP = 128
KEEP = 127 * STEP
CUT = KEEP - MAX_NEIGH * STEP
SCALE = 256.0
EPS = 1e-5
LAYERS = 5
COMBINE_AT, TURN_AT = 6, 28

ALU = mybir.AluOpType
ACT = mybir.ActivationFunctionType
AX = mybir.AxisListType.X
F32, F16, BF16 = mybir.dt.float32, mybir.dt.float16, mybir.dt.bfloat16
FP8, I16 = mybir.dt.float8e4, mybir.dt.int16

LN_OPS = 8


def build(nc, a):
    with ExitStack() as ctx:
        def sb(name, shape, dt=F32):
            return ctx.enter_context(nc.sbuf_tensor(name, shape, dt))

        def ps(name, shape):
            return ctx.enter_context(nc.psum_tensor(name, shape, F32))

        def sem(name):
            return ctx.enter_context(nc.semaphore(name))

        adjT = sb("adjT", [P, Q, JB, 2 * GC], FP8)
        xT = sb("xT", [D + 2, N])
        xrow = sb("xrow", [P, JB, D])
        hrow = sb("hrow", [P, JB, D])
        S = [sb(f"S{i}", [P, JB, 2 * D], F16) for i in range(2)]
        wgt = sb("wgt", [P, 2, 2, GC], I16)
        yT = sb("yT", [P, 2, GC])
        rz = sb("rz", [P, B, 2 * D])
        nn = sb("nn", [P, B, D])
        t1 = sb("t1", [P, B, D])
        t2 = sb("t2", [P, B, D])
        ts = sb("ts", [P, B, D])
        z = sb("z", [P, B, D])
        zc = sb("zc", [P, B, D])
        sq = sb("sq", [P, B, D])
        stat = sb("stat", [P, 4, B])
        rstd = sb("rstd", [P, B])
        mhalf = sb("mhalf", [P, JB])
        degrow = sb("degrow", [1, 2, GC])
        deg1 = sb("deg1", [P, JB])
        rdeg = sb("rdeg", [P, JB])
        dinv = sb("dinv", [P, JB])
        dinvS = sb("dinvS", [P, JB])
        consts = sb("consts", [P, 3 * P + D])
        tri = sb("tri", [P, P], BF16)
        fix = sb("fix", [P, P], BF16)
        eye8 = sb("eye8", [P, P], FP8)
        w_y = sb("w_y", [P, 2 * 3 * D + 2 * D])
        w_s = sb("w_s", [D, 3 * D])
        w_h = sb("w_h", [D + 2, 2, 4 * D])
        w_a = sb("w_a", [D, D])
        bias0 = sb("bias0", [P, D])
        one = sb("one", [1, 1])
        cutb = sb("cutb", [P, 1])

        identity = consts[:, 2 * P:3 * P]
        merge0 = consts[:, 3 * P:3 * P + D]

        V = [ps(f"V{c}", [P, GC]) for c in range(2)]
        Y = [ps(f"Y{c}", [P, GC]) for c in range(2)]
        gates = ps("gates", [P, B, 4 * D])
        turn = ps("turn", [P, GC])
        sup = ps("sup", [P, B, 2 * D])
        degcol = sup[:, :, D:D + G]
        rowsum = [gates[:, 2 * c, :].rearrange("p (b d) -> p b d", d=D) for c in range(2)]

        load = [sem(f"load{i}") for i in range(NLOAD)]
        small_in = sem("small_in")
        wh_zero = sem("wh_zero")
        wh_in = sem("wh_in")
        xT_in = sem("xT_in")
        const_ready = sem("const_ready")
        bias_added = sem("bias_added")
        v_done = [sem(f"v_done{c}") for c in range(2)]
        w_ready = [sem(f"w_ready{c}") for c in range(2)]
        v_total = [sem(f"v_total{c}") for c in range(2)]
        deg_ready = [sem(f"deg_ready{c}") for c in range(2)]
        degcol_done = sem("degcol_done")
        deg_step = sem("deg_step")
        dinv_pow = sem("dinv_pow")
        dinv_ready = sem("dinv_ready")
        y_done = sem("y_done")
        y_out = sem("y_out")
        combined = sem("combined")
        comb_read = sem("comb_read")
        rz_ready = sem("rz_ready")
        n_in = sem("n_in")
        n_ready = sem("n_ready")
        chain = sem("chain")
        var_ready = sem("var_ready")
        rstd_ready = sem("rstd_ready")
        rows_ready = sem("rows_ready")
        turned = sem("turned")
        xT_ready = sem("xT_ready")
        sup_done = sem("sup_done")
        hi_ready = sem("hi_ready")
        t_ready = sem("t_ready")
        s_ready = sem("s_ready")
        stored = sem("stored")

        def adj_tile(q, jb, c):
            return adjT[:, q, jb, c * GC:(c + 1) * GC]

        TURNS = {0: 0, 1: G, 3: 2 * G}
        SUPS = {-1: 0, 0: G, 1: 2 * G}
        SPLITS = {-1: 0, 0: G, 1: 2 * G, 2: 3 * G, 3: 4 * G}
        NSMALL = 11

        block = ctx.enter_context(nc.Block())

        @block.sync
        def _(sp):
            sp.dma_start(xT[0:D, :], a["xT"]).then_inc(xT_in, 16)
            sp.dma_start(consts[:, :], a["consts"]).then_inc(small_in, 16)
            for i, name in enumerate(("w0", "W1", "W2")):
                sp.dma_start(w_s[:, i * D:(i + 1) * D], a[name]).then_inc(small_in, 16)
            sp.dma_start(xrow[:, :, :], a["xrow"]).then_inc(small_in, 16)
            sp.dma_start(bias0[:, :], a["bias"].to_broadcast([P, D])).then_inc(small_in, 16)
            for half in range(2):
                rows = slice(half * D, (half + 1) * D)
                sp.dma_start(w_y[rows, 0:3 * D], a["wih1T"]).then_inc(small_in, 16)
                sp.dma_start(w_y[rows, 3 * D:6 * D], a["wih2T"]).then_inc(small_in, 16)
                sp.dma_start(w_y[rows, 6 * D:7 * D], a["L2W"]).then_inc(small_in, 16)
                sp.dma_start(w_y[rows, 7 * D:8 * D], a["L3WT"][D:2 * D, :]).then_inc(small_in, 16)
            sp.dma_start(w_a[:, :], a["L3WT"][0:D, :]).then_inc(small_in, 16)
            sp.wait_ge(wh_zero, 2)
            for l in range(2):
                sp.dma_start(w_h[0:D, l, 0:2 * D], a[f"whh{l + 1}T"][:, 0:2 * D]).then_inc(wh_in, 16)
                sp.dma_start(w_h[0:D, l, 3 * D:4 * D], a[f"whh{l + 1}T"][:, 2 * D:3 * D]).then_inc(wh_in, 16)
                sp.dma_start(w_h[D:D + 1, l, 0:3 * D], a[f"bih{l + 1}"]).then_inc(wh_in, 16)
                sp.dma_start(w_h[D + 1:D + 2, l, 0:2 * D], a[f"bhh{l + 1}"][:, 0:2 * D]).then_inc(wh_in, 16)
                sp.dma_start(w_h[D + 1:D + 2, l, 3 * D:4 * D], a[f"bhh{l + 1}"][:, 2 * D:3 * D]).then_inc(wh_in, 16)
            for g in range(G):
                sp.wait_ge(rows_ready, 4 * G + g + 1)
                sp.dma_start(a["out"][g], xrow[:, g * B:(g + 1) * B, :]).then_inc(stored, 16)
            sp.wait_ge(stored, 16 * G)

        @block.gpsimd
        def _(pool):
            def rsqrt_rows(e):
                pool.wait_ge(var_ready, e + 1)
                nc.gpsimd.tensor_tensor(rstd[:, :], stat[:, 3, :], mhalf[:, 0:B], ALU.pow).then_inc(rstd_ready, 1)

            for q in range(Q):
                for n in range(JP):
                    i = q * JP + n
                    if i >= NLOAD:
                        pool.wait_ge(load[i % NLOAD], 16 * (i // NLOAD))
                    jp = JP - 1 - n
                    pool.dma_start(adjT[:, q, 2 * jp:2 * jp + 2, :], a["adjT"][q, jp]).then_inc(load[i % NLOAD], 16)
                    if i == 1:
                        pool.wait_ge(small_in, 16 * (6 + 9))
                        nc.gpsimd.tensor_tensor(xrow[:, :, :], xrow[:, :, :],
                                                bias0[:, None, :].to_broadcast([P, JB, D]), ALU.add).then_inc(bias_added, 1)
                    if i == 2:
                        pool.wait_ge(const_ready, 5)
                    if q >= 1 and n == 13:
                        rsqrt_rows(2 * q - 2)
                    if q >= 2 and n == 5:
                        rsqrt_rows(2 * q - 3)
            rsqrt_rows(2 * Q - 3)
            pool.wait_ge(deg_step, 1)
            nc.gpsimd.tensor_tensor(dinv[:, :], deg1[:, :], mhalf[:, :], ALU.pow).then_inc(dinv_pow, 1)
            rsqrt_rows(2 * Q - 2)
            rsqrt_rows(2 * Q - 1)
            for e in range(G, 4 * G):
                rsqrt_rows(e)

        @block.scalar
        def _(act):
            def take_y(e):
                act.wait_ge(y_done, e + 1)
                if not isinstance(e, int) or e >= 2:
                    act.wait_ge(combined, e - 1)
                nc.scalar.activation(yT[:, e % 2, :], Y[e % 2][:, :], ACT.Copy).then_inc(y_out, 1)

            def take_xT(layer, g):
                act.wait_ge(turned, TURNS[layer] + g + 1)
                nc.scalar.activation(xT[0:D, g * GC:(g + 1) * GC], turn[0:D, :], ACT.Copy).then_inc(xT_ready, 1)

            def hi_of_support(layer, g):
                act.wait_ge(sup_done, SUPS[layer] + (G - g if layer < 0 else g + 1))
                nc.scalar.activation(S[(layer + 1) % 2][:, g * B:(g + 1) * B, 0:D], sup[:, :, 0:D], ACT.Copy)\
                    .then_inc(hi_ready, 1)

            def hi_of_rows(layer, g):
                act.wait_ge(t_ready, (layer - 2) * G + g + 1)
                nc.scalar.activation(S[(layer + 1) % 2][:, g * B:(g + 1) * B, 0:D], ts[:, :, :], ACT.Copy)\
                    .then_inc(hi_ready, 1)

            for g in range(G - 1, -1, -1):
                hi_of_support(-1, g)
            for q in range(Q):
                for t in range(JB):
                    act.wait_ge(v_done[0], q * JB + t + 1)
                    nc.scalar.activation(wgt[:, 0, t % 2, :], V[0][:, :], ACT.Relu, bias=cutb[:, 0:1])\
                        .then_inc(w_ready[0], 1)
                    if q >= 1:
                        if t == 0:
                            take_y(2 * q - 2)
                            take_y(2 * q - 1)
                        if t == 13:
                            take_xT(0, 2 * q - 2)
                        if t == 15:
                            hi_of_support(0, 2 * q - 2)
                        if t == 28:
                            take_xT(0, 2 * q - 1)
                        if t == 30:
                            hi_of_support(0, 2 * q - 1)
                act.wait_ge(v_total[0], q + 1)
                if q >= 1:
                    act.wait_ge(degcol_done, q)
                nc.scalar.activation(degrow[:, 0, :], V[0][0:1, :], ACT.Copy).then_inc(deg_ready[0], 1)
            for e in (G - 2, G - 1):
                take_y(e)
            for e in (G - 2, G - 1):
                take_xT(0, e)
                hi_of_support(0, e)
            for layer in range(1, LAYERS):
                for g in range(G):
                    e = layer * G + g
                    take_y(e)
                    if layer in (1, 2):
                        act.wait_ge(combined, e + 1)
                        nc.scalar.activation(rz[:, :, :], gates[:, :, 0:2 * D], ACT.Sigmoid).then_inc(rz_ready, 1)
                        act.wait_ge(n_in, e - G + 1)
                        nc.scalar.activation(nn[:, :, :], t2[:, :, :], ACT.Tanh).then_inc(n_ready, 1)
                    if layer == 1:
                        take_xT(1, g)
                        hi_of_support(1, g)
                    if layer == 2:
                        hi_of_rows(2, g)
                    if layer == 3:
                        hi_of_rows(3, g)
                        take_xT(3, g)

        @block.vector
        def _(dve):
            steps = [0]

            def did(ins):
                steps[0] += 1
                ins.then_inc(chain, 1)

            def after():
                dve.wait_ge(chain, steps[0])

            def norm_step(k, e, dst):
                if k < 7:
                    after()
                if k == 0:
                    did(nc.vector.tensor_reduce(stat[:, 0, :], z[:, :, :], AX, ALU.add))
                if k == 1:
                    did(nc.vector.tensor_scalar(stat[:, 1, :], stat[:, 0, :], -1.0 / D, None, ALU.mult))
                if k == 2:
                    did(nc.vector.tensor_tensor(zc[:, :, :], z[:, :, :],
                                                stat[:, 1, :, None].to_broadcast([P, B, D]), ALU.add))
                if k == 3:
                    did(nc.vector.tensor_tensor(sq[:, :, :], zc[:, :, :], zc[:, :, :], ALU.mult))
                if k == 4:
                    did(nc.vector.tensor_reduce(stat[:, 2, :], sq[:, :, :], AX, ALU.add))
                if k == 5:
                    nc.vector.tensor_scalar(stat[:, 3, :], stat[:, 2, :], 1.0 / D, EPS, ALU.mult, ALU.add)\
                        .then_inc(var_ready, 1)
                if k == 6:
                    pass
                if k == 7:
                    dve.wait_ge(rstd_ready, e + 1)
                    nc.vector.tensor_tensor(dst, zc[:, :, :], rstd[:, :, None].to_broadcast([P, B, D]), ALU.mult)\
                        .then_inc(rows_ready, 1)

            def rows0(e, k):
                grp = xrow[:, e * B:(e + 1) * B, :]
                if k == 0:
                    if e == 0:
                        dve.wait_ge(bias_added, 1)
                    dve.wait_ge(combined, e + 1)
                    did(nc.vector.tensor_tensor(z[:, :, :], rowsum[e % 2], grp, ALU.add))
                    after()
                elif k <= LN_OPS:
                    norm_step(k - 1, e, grp)

            def lo_of_support(layer, g):
                n = SPLITS[layer] + (G - g if layer < 0 else g + 1)
                dve.wait_ge(hi_ready, n)
                s = S[(layer + 1) % 2][:, g * B:(g + 1) * B, :]
                nc.vector.tensor_tensor(s[:, :, D:2 * D], sup[:, :, 0:D], s[:, :, 0:D], ALU.subtract)\
                    .then_inc(s_ready, 1)

            def split_rows(layer, g):
                dve.wait_ge(hi_ready, SPLITS[layer] + g + 1)
                s = S[(layer + 1) % 2][:, g * B:(g + 1) * B, :]
                nc.vector.tensor_tensor(s[:, :, D:2 * D], ts[:, :, :], s[:, :, 0:D], ALU.subtract)\
                    .then_inc(s_ready, 1)

            nc.vector.memset(w_h[:, :, :], 0.0).then_inc(wh_zero, 1)
            nc.vector.memset(xT[D:D + 2, :], 1.0).then_inc(wh_zero, 1)
            nc.vector.memset(mhalf[:, :], -0.5).then_inc(const_ready, 1)
            nc.vector.memset(one[:, :], 1.0).then_inc(const_ready, 1)
            nc.vector.memset(cutb[:, :], -float(CUT)).then_inc(const_ready, 1)
            dve.wait_ge(small_in, 16 * (6 + 9))
            nc.vector.tensor_scalar(w_s[:, :], w_s[:, :], SCALE, None, ALU.mult).then_inc(const_ready, 1)
            nc.vector.tensor_copy(tri[:, :], consts[:, 0:P]).then_inc(const_ready, 1)
            nc.vector.tensor_copy(fix[:, :], consts[:, P:2 * P]).then_inc(const_ready, 1)
            nc.vector.tensor_copy(eye8[:, :], consts[:, 2 * P:3 * P], saturate=False).then_inc(const_ready, 1)
            nc.vector.tensor_scalar(w_y[:, :], w_y[:, :], 1.0 / SCALE, None, ALU.mult).then_inc(const_ready, 1)
            for g in range(G - 1, -1, -1):
                lo_of_support(-1, g)
            for q in range(Q):
                for t in range(JB):
                    dve.wait_ge(v_done[1], q * JB + t + 1)
                    nc.vector.tensor_scalar(wgt[:, 1, t % 2, :], V[1][:, :], -float(CUT), 0.0, ALU.add, ALU.max)\
                        .then_inc(w_ready[1], 1)
                    if q >= 1:
                        if 2 <= t < 11:
                            rows0(2 * q - 2, t - 2)
                        if t == 16:
                            lo_of_support(0, 2 * q - 2)
                        if 17 <= t < 26:
                            rows0(2 * q - 1, t - 17)
                        if t == 31:
                            lo_of_support(0, 2 * q - 1)
                dve.wait_ge(v_total[1], q + 1)
                if q >= 1:
                    dve.wait_ge(degcol_done, q)
                nc.vector.tensor_copy(degrow[:, 1, :], V[1][0:1, :]).then_inc(deg_ready[1], 1)
            dve.wait_ge(degcol_done, Q)
            nc.vector.tensor_scalar(deg1[:, :].rearrange("p (g b) -> p b g", b=B), degcol, -1.0 / STEP, 1.0, ALU.mult, ALU.add).then_inc(deg_step, 1)
            dve.wait_ge(deg_step, 1)
            nc.vector.reciprocal(rdeg[:, :], deg1[:, :]).then_inc(dinv_ready, 1)
            dve.wait_ge(dinv_pow, 1)
            nc.vector.tensor_scalar(dinvS[:, :], dinv[:, :], SCALE, None, ALU.mult).then_inc(dinv_ready, 1)
            for e in (G - 2, G - 1):
                for k in range(LN_OPS + 1):
                    rows0(e, k)
                lo_of_support(0, e)
            dve.wait_ge(dinv_ready, 2)

            def gated(layer, g, old):
                e = layer * G + g
                dve.wait_ge(rz_ready, e - G + 1)
                did(nc.vector.tensor_tensor(t1[:, :, :], rz[:, :, 0:D], gates[:, :, 3 * D:4 * D], ALU.mult))
                after()
                nc.vector.tensor_tensor(t2[:, :, :], t1[:, :, :], gates[:, :, 2 * D:3 * D], ALU.add).then_inc(n_in, 1)
                dve.wait_ge(n_ready, e - G + 1)
                did(nc.vector.tensor_tensor(t1[:, :, :], old, nn[:, :, :], ALU.subtract))
                after()
                did(nc.vector.tensor_tensor(t2[:, :, :], t1[:, :, :], rz[:, :, D:2 * D], ALU.mult))
                after()
                did(nc.vector.tensor_tensor(z[:, :, :], t2[:, :, :], nn[:, :, :], ALU.add))
                after()

            for layer in range(1, LAYERS):
                for g in range(G):
                    e = layer * G + g
                    blk = slice(g * B, (g + 1) * B)
                    if layer == 1:
                        gated(1, g, xrow[:, blk, :])
                        nc.vector.tensor_scalar(hrow[:, blk, :], z[:, :, :], 0.0, None, ALU.max).then_inc(rows_ready, 1)
                        lo_of_support(1, g)
                        continue
                    if layer == 2:
                        gated(2, g, hrow[:, blk, :])
                        did(nc.vector.scalar_tensor_tensor(out=z[:, :, :], in0=z[:, :, :], scalar=0.0,
                                                           in1=xrow[:, blk, :], op0=ALU.max, op1=ALU.add))
                    if layer == 3:
                        dve.wait_ge(combined, e + 1)
                        did(nc.vector.tensor_tensor(t2[:, :, :], rowsum[0],
                                                    dinv[:, blk, None].to_broadcast([P, B, D]), ALU.mult))
                        after()
                        did(nc.vector.tensor_tensor(z[:, :, :], t2[:, :, :], xrow[:, blk, :], ALU.add))
                    if layer == 4:
                        dve.wait_ge(combined, e + 1)
                        did(nc.vector.tensor_tensor(t2[:, :, :], rowsum[0],
                                                    rdeg[:, blk, None].to_broadcast([P, B, D]), ALU.mult))
                        after()
                        did(nc.vector.tensor_tensor(t1[:, :, :], t2[:, :, :], rowsum[1], ALU.add))
                        after()
                        did(nc.vector.tensor_tensor(z[:, :, :], t1[:, :, :], xrow[:, blk, :], ALU.add))
                    for k in range(LN_OPS):
                        norm_step(k, e - G, xrow[:, blk, :])
                    if layer < 4:
                        dve.wait_ge(rows_ready, e + 1)
                        if layer == 2:
                            nc.vector.tensor_tensor(ts[:, :, :], xrow[:, blk, :],
                                                    dinvS[:, blk, None].to_broadcast([P, B, D]), ALU.mult)\
                                .then_inc(t_ready, 1)
                        else:
                            nc.vector.tensor_scalar(ts[:, :, :], xrow[:, blk, :], SCALE, None, ALU.mult)\
                                .then_inc(t_ready, 1)
                        split_rows(layer, g)

        @block.tensor
        def _(pe):
            def support(layer, g):
                if layer < 0:
                    if g < G - 1:
                        pe.wait_ge(s_ready, G - 1 - g)
                else:
                    pe.wait_ge(xT_ready, TURNS[layer] + g + 1)
                    pe.wait_ge(s_ready, SPLITS[layer] + g)
                for b in range(B):
                    c0 = g * GC + b * P
                    mm = nc.tensor.matmul(sup[:, b, 0:D], xT[0:D, c0:c0 + P],
                                          w_s[:, (layer + 1) * D:(layer + 2) * D], start=True, stop=True)
                mm.then_inc(sup_done, 1)

            def transpose_rows(layer, g):
                rows = hrow if layer == 1 else xrow
                pe.wait_ge(rows_ready, layer * G + g + 1)
                n = TURNS[layer] + g
                if not isinstance(n, int) or n > 0:
                    pe.wait_ge(xT_ready, n)
                for b in range(B):
                    mm = nc.tensor.transpose(turn[0:D, b * P:(b + 1) * P], rows[:, g * B + b, :], identity)
                mm.then_inc(turned, 1)

            def combine(layer, g):
                e = layer * G + g
                pe.wait_ge(y_out, e + 1)
                if layer == 0:
                    if not isinstance(e, int) or e >= 1:
                        pe.wait_ge(rows_ready, e)
                else:
                    pe.wait_ge(rows_ready, e)
                if layer == 4:
                    pe.wait_ge(xT_ready, TURNS[3] + g + 1)
                for b in range(B):
                    c0 = g * GC + b * P
                    y = yT[:, g % 2, b * P:(b + 1) * P]
                    if layer == 0:
                        mm = nc.tensor.matmul(rowsum[g % 2][:, b, :], y, merge0, start=True, stop=True)
                    if layer in (1, 2):
                        l = layer - 1
                        nc.tensor.matmul(gates[:, b, :], xT[:, c0:c0 + P], w_h[:, l, :], start=True, stop=True,
                                         skip_group_check=True)
                        mm = nc.tensor.matmul(gates[:, b, 0:3 * D], y, w_y[:, l * 3 * D:(l + 1) * 3 * D],
                                              start=False, stop=True, skip_group_check=True)
                    if layer == 3:
                        mm = nc.tensor.matmul(rowsum[0][:, b, :], y, w_y[:, 6 * D:7 * D], start=True, stop=True)
                    if layer == 4:
                        nc.tensor.matmul(rowsum[0][:, b, :], y, w_y[:, 7 * D:8 * D], start=True, stop=True)
                        mm = nc.tensor.matmul(rowsum[1][:, b, :], xT[0:D, c0:c0 + P], w_a[:, :], start=True, stop=True)
                mm.then_inc(combined, 1)

            def finish(layer, g):
                if layer in (0, 1, 3):
                    transpose_rows(layer, g)
                if layer in (0, 1):
                    support(layer, g)

            def weigh(q, t, c):
                if t == 0 and q >= 1:
                    pe.wait_ge(y_out, 2 * (q - 1) + c + 1)
                jb = JB - 1 - t
                if q == 0 and t % B == 0:
                    pe.wait_ge(s_ready, t // B + 1)
                mm = nc.tensor.matmul(Y[c][:, :], S[0][:, jb, :], wgt[:, c, t % 2, :].bitcast(BF16),
                                      start=(t == 0), stop=(t == JB - 1), skip_group_check=True)
                if t == JB - 1:
                    mm.then_inc(y_done, 1)

            def degrees(q):
                pe.wait_ge(s_ready, G + 2 * q)
                for c in range(2):
                    pe.wait_ge(deg_ready[c], q + 1)
                    for b in range(B):
                        mm = nc.tensor.matmul(degcol[:, b, 2 * q + c:2 * q + c + 1],
                                              degrow[:, c, b * P:(b + 1) * P], one[:, :], start=True, stop=True)
                mm.then_inc(degcol_done, 1)

            pe.wait_ge(xT_in, 16)
            pe.wait_ge(const_ready, 8)
            for g in range(G - 1, -1, -1):
                support(-1, g)
            for q in range(Q):
                for t in range(JB):
                    jb = JB - 1 - t
                    if t % 2 == 0:
                        i = q * JP + t // 2
                        pe.wait_ge(load[i % NLOAD], 16 * (i // NLOAD + 1))
                    for c in range(2):
                        if t == 0:
                            if q >= 1:
                                pe.wait_ge(deg_ready[c], q)
                        else:
                            pe.wait_ge(w_ready[c], q * JB + t)
                            nc.tensor.matmul(V[c][:, :], fix[:, :], adj_tile(q, jb + 1, c), start=False, stop=False,
                                             skip_group_check=True)
                        nc.tensor.matmul(V[c][:, :], tri[:, :], adj_tile(q, jb, c), start=(t == 0), stop=False,
                                         skip_group_check=True).then_inc(v_done[c], 1)
                        if t >= 1:
                            weigh(q, t - 1, c)
                    if q >= 1:
                        if t == 3:
                            degrees(q - 1)
                        if t == 1:
                            combine(0, 2 * q - 2)
                        if t == 12:
                            transpose_rows(0, 2 * q - 2)
                        if t == 14:
                            support(0, 2 * q - 2)
                        if t == 13:
                            combine(0, 2 * q - 1)
                        if t == 27:
                            transpose_rows(0, 2 * q - 1)
                        if t == 29:
                            support(0, 2 * q - 1)
                for c in range(2):
                    pe.wait_ge(w_ready[c], (q + 1) * JB)
                    nc.tensor.matmul(V[c][:, :], fix[:, :], adj_tile(q, 0, c), start=False, stop=True,
                                     skip_group_check=True).then_inc(v_total[c], 1)
                    weigh(q, JB - 1, c)
            degrees(Q - 1)
            combine(0, G - 2)
            transpose_rows(0, G - 2)
            pe.wait_ge(deg_step, 1)
            support(0, G - 2)
            combine(0, G - 1)
            finish(0, G - 1)
            pe.wait_ge(wh_in, 16 * 10)
            for layer in range(1, LAYERS):
                for g in range(G):
                    e = layer * G + g
                    pe.wait_ge(y_out, e - 1)
                    for jb in range(JB):
                        if g == 0 and jb % B == 0:
                            pe.wait_ge(s_ready, SPLITS[layer - 1] + jb // B + 1)
                        if jb == COMBINE_AT and e > G:
                            combine((e - 1) // G, (e - 1) % G)
                        if jb == TURN_AT - B and e > G and g == 0 or jb == TURN_AT and g > 0:
                            finish((e - 1) // G, (e - 1) % G)
                        last = jb == JB - 1
                        mm = nc.tensor.matmul(Y[g % 2][:, :], S[layer % 2][:, jb, :], adj_tile(g // 2, jb, g % 2),
                                              start=(jb == 0), stop=last and layer != 3, skip_group_check=True)
                    if layer == 3:
                        for b in range(B):
                            mm = nc.tensor.matmul(Y[g % 2][:, b * P:(b + 1) * P], S[1][:, g * B + b, :], eye8[:, :],
                                                  start=False, stop=(b == B - 1), skip_group_check=True)
                    mm.then_inc(y_done, 1)
            combine(LAYERS - 1, G - 1)


def kernel(x, adj, L0_gnn_weight, L0_gnn_bias, L1_gnn_W1, L1_gnn_wih1, L1_gnn_whh1, L1_gnn_bih1, L1_gnn_bhh1,
           L1_gnn_W2, L1_gnn_wih2, L1_gnn_whh2, L1_gnn_bih2, L1_gnn_bhh2, L2_gnn_W, L3_gnn_W):
    import numpy as np
    import concourse.bacc as bacc
    from concourse.bass_utils import run_bass_kernel_spmd

    def flat(v):
        return np.ascontiguousarray(v)

    x, adj = np.asarray(x), np.asarray(adj)
    behind = np.tril(np.ones((P, P), np.float32), -1)
    eye = np.eye(P, dtype=np.float32)
    tri = KEEP * eye - STEP * behind
    merge0 = np.concatenate([eye[0:D, 0:D]] * 2) * np.float32(2.0 ** (127 - MAX_NEIGH) / SCALE)
    arrays = {
        "adjT": flat(adj.reshape(Q, 2 * GC, JP, 2, P).transpose(0, 2, 4, 3, 1)).reshape(Q, JP, P, 4 * GC),
        "xT": flat(x.T),
        "xrow": flat(x.reshape(JB, P, D).transpose(1, 0, 2)),
        "consts": flat(np.concatenate([tri, -STEP - tri, eye, merge0], axis=1)),
        "w0": flat(L0_gnn_weight), "bias": flat(np.asarray(L0_gnn_bias).reshape(1, D)),
        "W1": flat(L1_gnn_W1), "W2": flat(L1_gnn_W2),
        "wih1T": flat(np.asarray(L1_gnn_wih1).T), "wih2T": flat(np.asarray(L1_gnn_wih2).T),
        "whh1T": flat(np.asarray(L1_gnn_whh1).T), "whh2T": flat(np.asarray(L1_gnn_whh2).T),
        "bih1": flat(np.asarray(L1_gnn_bih1).reshape(1, 3 * D)), "bhh1": flat(np.asarray(L1_gnn_bhh1).reshape(1, 3 * D)),
        "bih2": flat(np.asarray(L1_gnn_bih2).reshape(1, 3 * D)), "bhh2": flat(np.asarray(L1_gnn_bhh2).reshape(1, 3 * D)),
        "L2W": flat(L2_gnn_W), "L3WT": flat(np.asarray(L3_gnn_W).T),
    }
    nc = bacc.Bacc("TRN2", target_bir_lowering=False, num_devices=1)
    aps = {n: nc.dram_tensor(f"in_{n}", v.shape, mybir.dt.from_np(v.dtype), kind="ExternalInput").ap()
           for n, v in arrays.items()}
    aps["out"] = nc.dram_tensor("out_rows", (G, P, B * D), F32, kind="ExternalOutput").ap()
    build(nc, aps)
    r = run_bass_kernel_spmd(nc, [{f"in_{n}": v for n, v in arrays.items()}], core_ids=[0])
    rows = r.results[0]["out_rows"]
    return flat(rows.reshape(G, P, B, D).transpose(0, 2, 1, 3)).reshape(N, D)
```

```python
from contextlib import ExitStack

import concourse.bass as bass
from concourse import mybir

N, D = 4096, 64
P = 128
JB = N // P
GC = 512
G = N // GC
B = GC // P
Q = G // 2
JP = JB // 2
NLOAD = 16
MAX_NEIGH = 100
STEP = 128
KEEP = 127 * STEP
CUT = KEEP - MAX_NEIGH * STEP
SCALE = 256.0
EPS = 1e-5
LAYERS = 5
EARLY = JB - 2 * GC // P

ALU = mybir.AluOpType
ACT = mybir.ActivationFunctionType
AX = mybir.AxisListType.X
F32, F16, BF16 = mybir.dt.float32, mybir.dt.float16, mybir.dt.bfloat16
FP8, I16 = mybir.dt.float8e4, mybir.dt.int16

LN_OPS = 8


def build(nc, a):
    with ExitStack() as ctx:
        def sb(name, shape, dt=F32):
            return ctx.enter_context(nc.sbuf_tensor(name, shape, dt))

        def ps(name, shape):
            return ctx.enter_context(nc.psum_tensor(name, shape, F32))

        def sem(name):
            return ctx.enter_context(nc.semaphore(name))

        adjT = sb("adjT", [P, Q, JB, 2 * GC], FP8)
        xm = sb("xm", [P, N])
        xrow = sb("xrow", [P, JB, D])
        hrow = sb("hrow", [P, JB, D])
        S = [sb(f"S{i}", [P, JB, 2 * D], F16) for i in range(2)]
        wgt = sb("wgt", [P, 2, 2, GC], I16)
        yT = sb("yT", [P, 2, GC])
        rz = sb("rz", [P, B, 2 * D])
        nn = sb("nn", [P, B, D])
        t1 = sb("t1", [P, B, D])
        t2 = sb("t2", [P, B, D])
        ts = sb("ts", [P, B, D])
        z = sb("z", [P, B, D])
        zc = sb("zc", [P, B, D])
        sq = sb("sq", [P, B, D])
        stat = sb("stat", [P, 4, B])
        rstd = sb("rstd", [P, B])
        mhalf = sb("mhalf", [P, JB])
        ones = sb("ones", [P, GC], BF16)
        cutw = sb("cutw", [P, P], BF16)
        degrow = sb("degrow", [1, 2, GC])
        deg1 = sb("deg1", [P, JB])
        rdeg = sb("rdeg", [P, JB])
        dinv = sb("dinv", [P, JB])
        dinvS = sb("dinvS", [P, JB])
        consts = sb("consts", [P, 3 * P + D])
        tri = sb("tri", [P, P], BF16)
        fix = sb("fix", [P, P], BF16)
        eye8 = sb("eye8", [P, P], FP8)
        w_y = sb("w_y", [P, 2 * D])
        w_s = sb("w_s", [D, 3 * D])
        w_g = sb("w_g", [P, 2, 4 * D])
        brow = rz[0:2, :, :].rearrange("p b d -> p (b d)").rearrange("p (l c) -> p l c", l=2)
        b16 = sb("b16", [34, 2, 4 * D], F16)
        w_a = sb("w_a", [D, D])
        bias0 = sb("bias0", [P, D])
        one = sb("one", [1, 1])

        identity = consts[:, 2 * P:3 * P]
        merge0 = consts[:, 3 * P:3 * P + D]

        V = [ps(f"V{c}", [P, GC]) for c in range(2)]
        Y = [ps(f"Y{c}", [P, GC]) for c in range(2)]
        gates = ps("gates", [P, B, 4 * D])
        turn = ps("turn", [P, GC])
        sup = ps("sup", [P, B, 2 * D])
        degcol = sup[:, :, D:D + G]
        rowsum = [gates[:, 2 * c, :].rearrange("p (b d) -> p b d", d=D) for c in range(2)]

        load = [sem(f"load{i}") for i in range(NLOAD)]
        small_in = sem("small_in")
        gate_zero = sem("gate_zero")
        gate_in = sem("gate_in")
        gate_const = sem("gate_const")
        xT_in = [sem(f"xT_in{g}") for g in range(G)]
        ws_in = sem("ws_in")
        consts_in = sem("consts_in")
        const_ready = sem("const_ready")
        bias_added = sem("bias_added")
        v_done = [sem(f"v_done{c}") for c in range(2)]
        w_ready = [sem(f"w_ready{c}") for c in range(2)]
        v_total = [sem(f"v_total{c}") for c in range(2)]
        deg_ready = [sem(f"deg_ready{c}") for c in range(2)]
        degcol_done = sem("degcol_done")
        deg_step = sem("deg_step")
        dinv_pow = sem("dinv_pow")
        dinv_ready = sem("dinv_ready")
        y_done = sem("y_done")
        y_half = sem("y_half")
        y_out = sem("y_out")
        combined = sem("combined")
        sums_read = sem("sums_read")
        rz_ready = sem("rz_ready")
        n_in = sem("n_in")
        n_ready = sem("n_ready")
        chain = sem("chain")
        var_ready = sem("var_ready")
        rstd_ready = sem("rstd_ready")
        rows_ready = sem("rows_ready")
        turned = sem("turned")
        xT_ready = sem("xT_ready")
        sup_done = sem("sup_done")
        hi_ready = sem("hi_ready")
        t_ready = sem("t_ready")
        s_ready = sem("s_ready")
        stored = sem("stored")

        def adj_tile(q, jb, c):
            return adjT[:, q, jb, c * GC:(c + 1) * GC]

        TURNS = {0: 0, 1: G, 3: 2 * G}
        SUPS = {-1: 0, 0: G, 1: 2 * G}
        SPLITS = {-1: 0, 0: G, 1: 2 * G, 2: 3 * G, 3: 4 * G}
        CONSTS = 9

        block = ctx.enter_context(nc.Block())

        @block.sync
        def _(sp):
            for i, name in enumerate(("w0", "W1", "W2")):
                sp.dma_start(w_s[:, i * D:(i + 1) * D], a[name]).then_inc(ws_in, 16)
            for g in range(G - 1, -1, -1):
                sp.dma_start(xm[0:D, g * GC:(g + 1) * GC], a["xT"][:, g * GC:(g + 1) * GC]).then_inc(xT_in[g], 16)
            sp.dma_start(xrow[:, :, :], a["xrow"]).then_inc(small_in, 16)
            sp.dma_start(bias0[:, :], a["bias"].to_broadcast([P, D])).then_inc(small_in, 16)
            for half in range(2):
                rows = slice(half * D, (half + 1) * D)
                sp.dma_start(w_y[rows, 0:D], a["L2W"]).then_inc(small_in, 16)
                sp.dma_start(w_y[rows, D:2 * D], a["L3WT"][D:2 * D, :]).then_inc(small_in, 16)
            sp.dma_start(w_a[:, :], a["L3WT"][0:D, :]).then_inc(small_in, 16)
            sp.wait_ge(gate_zero, 3)
            for l in range(2):
                for src, b, rows, at in (("whh", "bhh", slice(0, D), 3 * D), ("wih", "bih", slice(D, P), 2 * D)):
                    w, row = a[f"{src}{l + 1}T"], 1 if b == "bhh" else 0
                    sp.dma_start(w_g[rows, l, 0:2 * D], w[:, 0:2 * D]).then_inc(gate_in, 16)
                    sp.dma_start(w_g[rows, l, at:at + D], w[:, 2 * D:3 * D]).then_inc(gate_in, 16)
                    sp.dma_start(brow[row:row + 1, l, 0:2 * D], a[f"{b}{l + 1}"][:, 0:2 * D]).then_inc(gate_in, 16)
                    sp.dma_start(brow[row:row + 1, l, at:at + D], a[f"{b}{l + 1}"][:, 2 * D:3 * D]).then_inc(gate_in, 16)
            for g in range(G):
                sp.wait_ge(rows_ready, 4 * G + g + 1)
                sp.dma_start(a["out"][g], xrow[:, g * B:(g + 1) * B, :]).then_inc(stored, 16)
            sp.wait_ge(stored, 16 * G)

        @block.gpsimd
        def _(pool):
            def rsqrt_rows(e):
                pool.wait_ge(var_ready, e + 1)
                nc.gpsimd.tensor_tensor(rstd[:, :], stat[:, 3, :], mhalf[:, 0:B], ALU.pow).then_inc(rstd_ready, 1)

            for q in range(Q):
                for n in range(JP):
                    i = q * JP + n
                    if i >= NLOAD:
                        pool.wait_ge(load[i % NLOAD], 16 * (i // NLOAD))
                    jp = JP - 1 - n
                    pool.dma_start(adjT[:, q, 2 * jp:2 * jp + 2, :], a["adjT"][q, jp]).then_inc(load[i % NLOAD], 16)
                    if i == 6:
                        pool.wait_ge(const_ready, CONSTS)
                        pool.wait_ge(small_in, 16 * 7)
                        nc.gpsimd.tensor_tensor(xrow[:, :, :], xrow[:, :, :],
                                                bias0[:, None, :].to_broadcast([P, JB, D]), ALU.add).then_inc(bias_added, 1)
                    if q >= 1 and n == 13:
                        rsqrt_rows(2 * q - 2)
                    if q >= 2 and n == 5:
                        rsqrt_rows(2 * q - 3)
            rsqrt_rows(2 * Q - 3)
            pool.wait_ge(deg_step, 1)
            nc.gpsimd.tensor_tensor(dinv[:, :], deg1[:, :], mhalf[:, :], ALU.pow).then_inc(dinv_pow, 1)
            rsqrt_rows(2 * Q - 2)
            rsqrt_rows(2 * Q - 1)
            for e in range(G, 4 * G):
                rsqrt_rows(e)

        @block.scalar
        def _(act):
            act.dma_start(consts[:, :], a["consts"]).then_inc(consts_in, 16)

            def take_y(e):
                act.wait_ge(y_done, e + 1)
                act.wait_ge(combined, e - 1)
                if e // G in (1, 2):
                    nc.scalar.activation(yT[D:P, e % 2, :], Y[e % 2][0:D, :], ACT.Copy).then_inc(y_half, 1)
                else:
                    nc.scalar.activation(yT[:, e % 2, :], Y[e % 2][:, :], ACT.Copy).then_inc(y_out, 1)

            def take_xT(layer, g):
                act.wait_ge(turned, TURNS[layer] + g + 1)
                nc.scalar.activation(xm[0:D, g * GC:(g + 1) * GC], turn[0:D, :], ACT.Copy).then_inc(xT_ready, 1)

            def hi_of_support(layer, g):
                act.wait_ge(sup_done, SUPS[layer] + g + 1)
                nc.scalar.activation(S[(layer + 1) % 2][:, g * B:(g + 1) * B, 0:D], sup[:, :, 0:D], ACT.Copy)\
                    .then_inc(hi_ready, 1)

            def hi_of_rows(layer, g):
                act.wait_ge(t_ready, (layer - 2) * G + g + 1)
                nc.scalar.activation(S[(layer + 1) % 2][:, g * B:(g + 1) * B, 0:D], ts[:, :, :], ACT.Copy)\
                    .then_inc(hi_ready, 1)

            for q in range(Q):
                for t in range(JB):
                    for c in range(2):
                        act.wait_ge(v_done[c], q * JB + t + 1)
                        nc.scalar.activation(wgt[:, c, t % 2, :], V[c][:, :], ACT.Relu).then_inc(w_ready[c], 1)
                for c in range(2):
                    act.wait_ge(v_total[c], q + 1)
                    if q >= 1:
                        act.wait_ge(degcol_done, q)
                    nc.scalar.activation(degrow[:, c, :], V[c][0:1, :], ACT.Copy).then_inc(deg_ready[c], 1)

            def gate(layer, g):
                e = layer * G + g
                if layer in (1, 2):
                    act.wait_ge(combined, e + 1)
                    act.wait_ge(rows_ready, e)
                    nc.scalar.activation(rz[:, :, :], gates[:, :, 0:2 * D], ACT.Sigmoid).then_inc(rz_ready, 1)
                    act.wait_ge(n_in, e - G + 1)
                    nc.scalar.activation(nn[:, :, :], t2[:, :, :], ACT.Tanh).then_inc(n_ready, 1)
                if layer == 2 and 1 <= g < G - 1:
                    take_y(e + 1)
                if layer in (2, 3):
                    hi_of_rows(layer, g)

            def finish(layer, g):
                if layer in (1, 3):
                    take_xT(layer, g)
                if layer == 1:
                    hi_of_support(layer, g)

            for layer in range(1, LAYERS):
                take_y(layer * G)
                take_y(layer * G + 1)
                gate(layer, 0)
                finish(layer, 0)
                gate(layer, 1)
                for g in range(2, G):
                    if layer != 2:
                        take_y(layer * G + g)
                    finish(layer, g - 1)
                    gate(layer, g)
                finish(layer, G - 1)

        @block.vector
        def _(dve):
            steps = [0]

            def did(ins):
                steps[0] += 1
                ins.then_inc(chain, 1)

            def after():
                dve.wait_ge(chain, steps[0])

            def norm_step(k, e, dst, take=None):
                if k < 7:
                    after()
                if k == 0:
                    did(nc.vector.tensor_reduce(stat[:, 0, :], z[:, :, :], AX, ALU.add))
                if k == 1:
                    did(nc.vector.tensor_scalar(stat[:, 1, :], stat[:, 0, :], -1.0 / D, None, ALU.mult))
                if k == 2:
                    did(nc.vector.tensor_tensor(zc[:, :, :], z[:, :, :],
                                                stat[:, 1, :, None].to_broadcast([P, B, D]), ALU.add))
                if k == 3:
                    did(nc.vector.tensor_tensor(sq[:, :, :], zc[:, :, :], zc[:, :, :], ALU.mult))
                if k == 4:
                    did(nc.vector.tensor_reduce(stat[:, 2, :], sq[:, :, :], AX, ALU.add))
                if k == 5:
                    nc.vector.tensor_scalar(stat[:, 3, :], stat[:, 2, :], 1.0 / D, EPS, ALU.mult, ALU.add)\
                        .then_inc(var_ready, 1)
                if k == 6 and take is not None:
                    take_y(take)
                if k == 7:
                    dve.wait_ge(rstd_ready, e + 1)
                    nc.vector.tensor_tensor(dst, zc[:, :, :], rstd[:, :, None].to_broadcast([P, B, D]), ALU.mult)\
                        .then_inc(rows_ready, 1)

            def take_y(e):
                if e < G:
                    dve.wait_ge(y_done, e + 1)
                    if e >= 2:
                        dve.wait_ge(combined, e - 1)
                    nc.vector.tensor_copy(yT[:, e % 2, :], Y[e % 2][:, :]).then_inc(y_out, 1)
                elif e < 3 * G:
                    c0 = e % G * GC
                    dve.wait_ge(y_half, e - G + 1)
                    nc.vector.tensor_tensor(xm[D:P, c0:c0 + GC], Y[e % 2][D:P, :], yT[D:P, e % 2, :], ALU.add)\
                        .then_inc(y_out, 1)

            def take_xT(g):
                dve.wait_ge(turned, g + 1)
                nc.vector.tensor_copy(xm[0:D, g * GC:(g + 1) * GC], turn[0:D, :]).then_inc(xT_ready, 1)

            def rows0(e, k):
                grp = xrow[:, e * B:(e + 1) * B, :]
                if k == 0:
                    if e == 0:
                        dve.wait_ge(bias_added, 1)
                    dve.wait_ge(combined, e + 1)
                    did(nc.vector.tensor_tensor(z[:, :, :], rowsum[e % 2], grp, ALU.add))
                    after()
                elif k <= LN_OPS:
                    norm_step(k - 1, e, grp)

            def split_support(layer, g):
                n = SPLITS[layer] + (G - g if layer < 0 else g + 1)
                s = S[(layer + 1) % 2][:, g * B:(g + 1) * B, :]
                if layer <= 0:
                    dve.wait_ge(sup_done, n)
                    nc.vector.tensor_copy(s[:, :, 0:D], sup[:, :, 0:D]).then_inc(hi_ready, 1)
                dve.wait_ge(hi_ready, n)
                nc.vector.tensor_tensor(s[:, :, D:2 * D], sup[:, :, 0:D], s[:, :, 0:D], ALU.subtract)\
                    .then_inc(s_ready, 1)

            def split_rows(layer, g):
                dve.wait_ge(hi_ready, SPLITS[layer] + g + 1)
                s = S[(layer + 1) % 2][:, g * B:(g + 1) * B, :]
                nc.vector.tensor_tensor(s[:, :, D:2 * D], ts[:, :, :], s[:, :, 0:D], ALU.subtract)\
                    .then_inc(s_ready, 1)

            def layer0_groups(first):
                for e in (first, first + 1):
                    for k in range(LN_OPS + 1):
                        rows0(e, k)
                    take_xT(e)
                    split_support(0, e)

            nc.vector.memset(w_g[:, :, :], 0.0).then_inc(gate_zero, 1)
            nc.vector.memset(brow[:, :, :], 0.0).then_inc(gate_zero, 1)
            nc.vector.memset(b16[:, :, :], 0.0).then_inc(gate_zero, 1)
            nc.vector.memset(mhalf[:, :], -0.5).then_inc(const_ready, 1)
            nc.vector.memset(one[:, :], 1.0).then_inc(const_ready, 1)
            nc.vector.memset(cutw[:, :], -float(CUT) / P).then_inc(const_ready, 1)
            nc.vector.memset(ones[:, :], 1.0).then_inc(const_ready, 1)
            dve.wait_ge(ws_in, 16 * 3)
            nc.vector.tensor_scalar(w_s[:, :], w_s[:, :], SCALE, None, ALU.mult).then_inc(const_ready, 1)
            dve.wait_ge(consts_in, 16)
            nc.vector.tensor_copy(tri[:, :], consts[:, 0:P]).then_inc(const_ready, 1)
            nc.vector.tensor_copy(fix[:, :], consts[:, P:2 * P]).then_inc(const_ready, 1)
            nc.vector.tensor_copy(eye8[:, :], consts[:, 2 * P:3 * P], saturate=False).then_inc(const_ready, 1)
            split_support(-1, G - 1)
            dve.wait_ge(small_in, 16 * 7)
            nc.vector.tensor_scalar(w_y[:, :], w_y[:, :], 1.0 / SCALE, None, ALU.mult).then_inc(const_ready, 1)
            for g in range(G - 2, -1, -1):
                split_support(-1, g)
            dve.wait_ge(gate_in, 16 * 16)
            nc.vector.tensor_scalar(w_g[D:P, :, :], w_g[D:P, :, :], 1.0 / SCALE, None, ALU.mult).then_inc(gate_const, 1)
            nc.vector.tensor_copy(b16[0:2, :, :], brow[:, :, :]).then_inc(gate_const, 1)
            dve.wait_ge(gate_const, 2)
            nc.vector.tensor_tensor(b16[32:34, :, :], brow[:, :, :], b16[0:2, :, :], ALU.subtract).then_inc(gate_const, 1)
            for q in range(Q):
                if q >= 1:
                    take_y(2 * q - 2)
                    take_y(2 * q - 1)
                    layer0_groups(2 * q - 2)
            take_y(G - 2)
            take_y(G - 1)
            dve.wait_ge(degcol_done, Q)
            nc.vector.tensor_scalar(deg1[:, :].rearrange("p (g b) -> p b g", b=B), degcol, -1.0 / STEP, 1.0 - CUT / STEP, ALU.mult, ALU.add).then_inc(deg_step, 1)
            dve.wait_ge(deg_step, 1)
            nc.vector.reciprocal(rdeg[:, :], deg1[:, :]).then_inc(dinv_ready, 1)
            dve.wait_ge(dinv_pow, 1)
            nc.vector.tensor_scalar(dinvS[:, :], dinv[:, :], SCALE, None, ALU.mult).then_inc(dinv_ready, 1)
            layer0_groups(G - 2)
            dve.wait_ge(dinv_ready, 2)

            def gated(layer, g, old):
                e = layer * G + g
                dve.wait_ge(rz_ready, e - G + 1)
                did(nc.vector.tensor_tensor(t1[:, :, :], rz[:, :, 0:D], gates[:, :, 3 * D:4 * D], ALU.mult))
                after()
                nc.vector.tensor_tensor(t2[:, :, :], t1[:, :, :], gates[:, :, 2 * D:3 * D], ALU.add).then_inc(n_in, 1)
                dve.wait_ge(n_ready, e - G + 1)
                did(nc.vector.tensor_tensor(t1[:, :, :], old, nn[:, :, :], ALU.subtract))
                after()
                did(nc.vector.tensor_tensor(t2[:, :, :], t1[:, :, :], rz[:, :, D:2 * D], ALU.mult))
                after()
                did(nc.vector.tensor_tensor(z[:, :, :], t2[:, :, :], nn[:, :, :], ALU.add))
                after()

            for layer in range(1, LAYERS):
                for g in range(G):
                    e = layer * G + g
                    blk = slice(g * B, (g + 1) * B)
                    if layer in (1, 2) and g == 0:
                        take_y(e)
                        take_y(e + 1)
                    if layer == 1:
                        if g >= 2:
                            take_y(e)
                            split_support(1, g - 1)
                        gated(1, g, xrow[:, blk, :])
                        nc.vector.tensor_scalar(hrow[:, blk, :], z[:, :, :], 0.0, None, ALU.max).then_inc(rows_ready, 1)
                        if g in (0, G - 1):
                            split_support(1, g)
                        continue
                    if layer == 2:
                        gated(2, g, hrow[:, blk, :])
                        did(nc.vector.scalar_tensor_tensor(out=z[:, :, :], in0=z[:, :, :], scalar=0.0,
                                                           in1=xrow[:, blk, :], op0=ALU.max, op1=ALU.add))
                    if layer == 3:
                        dve.wait_ge(combined, e + 1)
                        nc.vector.tensor_tensor(t2[:, :, :], rowsum[0],
                                                dinv[:, blk, None].to_broadcast([P, B, D]), ALU.mult).then_inc(sums_read, 1)
                        dve.wait_ge(sums_read, g + 1)
                        did(nc.vector.tensor_tensor(z[:, :, :], t2[:, :, :], xrow[:, blk, :], ALU.add))
                    if layer == 4:
                        dve.wait_ge(combined, e + 1)
                        did(nc.vector.tensor_tensor(t2[:, :, :], rowsum[0],
                                                    rdeg[:, blk, None].to_broadcast([P, B, D]), ALU.mult))
                        after()
                        nc.vector.tensor_tensor(t1[:, :, :], t2[:, :, :], rowsum[1], ALU.add).then_inc(sums_read, 1)
                        dve.wait_ge(sums_read, G + g + 1)
                        did(nc.vector.tensor_tensor(z[:, :, :], t1[:, :, :], xrow[:, blk, :], ALU.add))
                    for k in range(LN_OPS):
                        norm_step(k, e - G, xrow[:, blk, :], e + 1 if layer == 2 and 1 <= g < G - 1 else None)
                    if layer < 4:
                        dve.wait_ge(rows_ready, e + 1)
                        if layer == 2:
                            nc.vector.tensor_tensor(ts[:, :, :], xrow[:, blk, :],
                                                    dinvS[:, blk, None].to_broadcast([P, B, D]), ALU.mult)\
                                .then_inc(t_ready, 1)
                        else:
                            nc.vector.tensor_scalar(ts[:, :, :], xrow[:, blk, :], SCALE, None, ALU.mult)\
                                .then_inc(t_ready, 1)
                        split_rows(layer, g)

        @block.tensor
        def _(pe):
            def support(layer, g):
                if layer < 0:
                    pe.wait_ge(xT_in[g], 16)
                    if g < G - 1:
                        pe.wait_ge(s_ready, G - 1 - g)
                else:
                    pe.wait_ge(xT_ready, TURNS[layer] + g + 1)
                    pe.wait_ge(s_ready, SPLITS[layer] + g)
                for b in range(B):
                    c0 = g * GC + b * P
                    mm = nc.tensor.matmul(sup[:, b, 0:D], xm[0:D, c0:c0 + P],
                                          w_s[:, (layer + 1) * D:(layer + 2) * D], start=True, stop=True)
                mm.then_inc(sup_done, 1)

            def transpose_rows(layer, g):
                rows = hrow if layer == 1 else xrow
                pe.wait_ge(rows_ready, layer * G + g + 1)
                n = TURNS[layer] + g
                if not isinstance(n, int) or n > 0:
                    pe.wait_ge(xT_ready, n)
                for b in range(B):
                    mm = nc.tensor.transpose(turn[0:D, b * P:(b + 1) * P], rows[:, g * B + b, :], identity)
                mm.then_inc(turned, 1)

            def combine(layer, g):
                e = layer * G + g
                pe.wait_ge(y_out, e + 1)
                if layer == 0:
                    if e >= 2:
                        pe.wait_ge(rows_ready, e - 1)
                elif e > G and layer in (1, 2):
                    pe.wait_ge(n_in, e - G)
                elif layer >= 3:
                    pe.wait_ge(sums_read, e - 3 * G) if e > 3 * G else pe.wait_ge(n_in, 2 * G)
                if layer == 4:
                    pe.wait_ge(xT_ready, TURNS[3] + g + 1)
                for b in range(B):
                    c0 = g * GC + b * P
                    y = yT[:, g % 2, b * P:(b + 1) * P]
                    if layer == 0:
                        mm = nc.tensor.matmul(rowsum[g % 2][:, b, :], y, merge0, start=True, stop=True)
                    if layer in (1, 2):
                        l = layer - 1
                        nc.tensor.matmul(gates[:, b, :], ones[0:34, 0:P], b16[:, l, :], start=True, stop=False)
                        mm = nc.tensor.matmul(gates[:, b, :], xm[:, c0:c0 + P], w_g[:, l, :], start=False, stop=True)
                    if layer == 3:
                        mm = nc.tensor.matmul(rowsum[0][:, b, :], y, w_y[:, 0:D], start=True, stop=True)
                    if layer == 4:
                        nc.tensor.matmul(rowsum[0][:, b, :], y, w_y[:, D:2 * D], start=True, stop=True)
                        mm = nc.tensor.matmul(rowsum[1][:, b, :], xm[0:D, c0:c0 + P], w_a[:, :], start=True, stop=True)
                mm.then_inc(combined, 1)

            def weigh(q, t, c):
                if t == 0 and q >= 1:
                    pe.wait_ge(y_out, 2 * (q - 1) + c + 1)
                jb = JB - 1 - t
                if q == 0 and t % B == 0:
                    pe.wait_ge(s_ready, t // B + 1)
                mm = nc.tensor.matmul(Y[c][:, :], S[0][:, jb, :], wgt[:, c, t % 2, :].bitcast(BF16),
                                      start=(t == 0), stop=(t == JB - 1), skip_group_check=True)
                if t == JB - 1:
                    mm.then_inc(y_done, 1)

            def degrees(q):
                pe.wait_ge(s_ready, G + 2 * q)
                for c in range(2):
                    pe.wait_ge(deg_ready[c], q + 1)
                    for b in range(B):
                        mm = nc.tensor.matmul(degcol[:, b, 2 * q + c:2 * q + c + 1],
                                              degrow[:, c, b * P:(b + 1) * P], one[:, :], start=True, stop=True)
                mm.then_inc(degcol_done, 1)

            pe.wait_ge(const_ready, CONSTS - 1)
            support(-1, G - 1)
            for q in range(Q):
                for t in range(JB):
                    jb = JB - 1 - t
                    if t % 2 == 0:
                        i = q * JP + t // 2
                        pe.wait_ge(load[i % NLOAD], 16 * (i // NLOAD + 1))
                    for c in range(2):
                        if t == 0:
                            if q >= 1:
                                pe.wait_ge(deg_ready[c], q)
                            nc.tensor.matmul(V[c][:, :], cutw[:, :], ones[:, :], start=True, stop=False,
                                             skip_group_check=True)
                        else:
                            pe.wait_ge(w_ready[c], q * JB + t)
                            nc.tensor.matmul(V[c][:, :], fix[:, :], adj_tile(q, jb + 1, c), start=False, stop=False,
                                             skip_group_check=True)
                        nc.tensor.matmul(V[c][:, :], tri[:, :], adj_tile(q, jb, c), start=False, stop=False,
                                         skip_group_check=True).then_inc(v_done[c], 1)
                        if t >= 1:
                            weigh(q, t - 1, c)
                    if q == 0 and t % B == 0 and t < JB - B:
                        support(-1, G - 2 - t // B)
                    if q >= 1:
                        if t == 3:
                            degrees(q - 1)
                        if t == 2:
                            combine(0, 2 * q - 2)
                        if t == 10:
                            transpose_rows(0, 2 * q - 2)
                        if t == 12:
                            support(0, 2 * q - 2)
                        if t == 13:
                            combine(0, 2 * q - 1)
                        if t == 22:
                            transpose_rows(0, 2 * q - 1)
                        if t == 24:
                            support(0, 2 * q - 1)
                for c in range(2):
                    pe.wait_ge(w_ready[c], (q + 1) * JB)
                    nc.tensor.matmul(V[c][:, :], fix[:, :], adj_tile(q, 0, c), start=False, stop=True,
                                     skip_group_check=True).then_inc(v_total[c], 1)
                    weigh(q, JB - 1, c)
            degrees(Q - 1)
            pe.wait_ge(gate_const, 3)
            pe.wait_ge(const_ready, CONSTS)

            def product(layer, g, first, last):
                if first == 0:
                    pe.wait_ge(y_out, layer * G + g - 1)
                for jb in range(first, last):
                    if g < 2 and jb % B == 0:
                        pe.wait_ge(s_ready, SPLITS[layer - 1] + jb // B + 1)
                    mm = nc.tensor.matmul(Y[g % 2][:, :], S[layer % 2][:, jb, :], adj_tile(g // 2, jb, g % 2),
                                          start=(jb == 0), stop=(jb == JB - 1), skip_group_check=True)
                if last == JB:
                    if layer == 3:
                        for b in range(B):
                            mm = nc.tensor.matmul(Y[g % 2][:, b * P:(b + 1) * P], S[1][:, g * B + b, :], eye8[:, :],
                                                  start=False, stop=True, skip_group_check=True)
                    mm.then_inc(y_done, 1)

            for layer in range(1, LAYERS):
                if layer == 1:
                    product(1, 0, 0, 4)
                    combine(0, G - 2)
                    product(1, 0, 4, 10)
                    combine(0, G - 1)
                    product(1, 0, 10, EARLY)
                    product(1, 1, 0, 2)
                    transpose_rows(0, G - 2)
                    product(1, 1, 2, 7)
                    pe.wait_ge(deg_step, 1)
                    support(0, G - 2)
                    product(1, 1, 7, 18)
                    transpose_rows(0, G - 1)
                    product(1, 1, 18, EARLY)
                    support(0, G - 1)
                else:
                    product(layer, 0, 0, 2)
                    if layer != 3:
                        transpose_rows(layer - 1, G - 2)
                    product(layer, 0, 2, 7)
                    if layer == 2:
                        support(layer - 1, G - 2)
                    product(layer, 0, 7, 12)
                    combine(layer - 1, G - 1)
                    product(layer, 0, 12, EARLY)
                    product(layer, 1, 0, 12)
                    if layer != 3:
                        transpose_rows(layer - 1, G - 1)
                    product(layer, 1, 12, 17)
                    if layer == 2:
                        support(layer - 1, G - 1)
                    product(layer, 1, 17, EARLY)
                product(layer, 0, EARLY, JB)
                product(layer, 1, EARLY, JB - 2)
                combine(layer, 0)
                product(layer, 1, JB - 2, JB)
                for g in range(2, G):
                    turn_at, support_at, combine_at = {2: (14, 19, 20), 3: (8, 13, 16)}.get(g, (4, 9, 16))
                    product(layer, g, 0, turn_at)
                    if layer in (1, 3):
                        transpose_rows(layer, g - 2)
                    product(layer, g, turn_at, support_at)
                    if layer == 1:
                        support(layer, g - 2)
                    product(layer, g, support_at, combine_at)
                    combine(layer, g - 1)
                    product(layer, g, combine_at, JB)
            combine(LAYERS - 1, G - 1)


def kernel(x, adj, L0_gnn_weight, L0_gnn_bias, L1_gnn_W1, L1_gnn_wih1, L1_gnn_whh1, L1_gnn_bih1, L1_gnn_bhh1,
           L1_gnn_W2, L1_gnn_wih2, L1_gnn_whh2, L1_gnn_bih2, L1_gnn_bhh2, L2_gnn_W, L3_gnn_W):
    import numpy as np
    import concourse.bacc as bacc
    from concourse.bass_utils import run_bass_kernel_spmd

    def flat(v):
        return np.ascontiguousarray(v)

    x, adj = np.asarray(x), np.asarray(adj)
    behind = np.tril(np.ones((P, P), np.float32), -1)
    eye = np.eye(P, dtype=np.float32)
    tri = KEEP * eye - STEP * behind
    merge0 = np.concatenate([eye[0:D, 0:D]] * 2) * np.float32(2.0 ** (127 - MAX_NEIGH) / SCALE)
    arrays = {
        "adjT": flat(adj.reshape(Q, 2 * GC, JP, 2, P).transpose(0, 2, 4, 3, 1)).reshape(Q, JP, P, 4 * GC),
        "xT": flat(x.T),
        "xrow": flat(x.reshape(JB, P, D).transpose(1, 0, 2)),
        "consts": flat(np.concatenate([tri, -STEP - tri, eye, merge0], axis=1)),
        "w0": flat(L0_gnn_weight), "bias": flat(np.asarray(L0_gnn_bias).reshape(1, D)),
        "W1": flat(L1_gnn_W1), "W2": flat(L1_gnn_W2),
        "wih1T": flat(np.asarray(L1_gnn_wih1).T), "wih2T": flat(np.asarray(L1_gnn_wih2).T),
        "whh1T": flat(np.asarray(L1_gnn_whh1).T), "whh2T": flat(np.asarray(L1_gnn_whh2).T),
        "bih1": flat(np.asarray(L1_gnn_bih1).reshape(1, 3 * D)), "bhh1": flat(np.asarray(L1_gnn_bhh1).reshape(1, 3 * D)),
        "bih2": flat(np.asarray(L1_gnn_bih2).reshape(1, 3 * D)), "bhh2": flat(np.asarray(L1_gnn_bhh2).reshape(1, 3 * D)),
        "L2W": flat(L2_gnn_W), "L3WT": flat(np.asarray(L3_gnn_W).T),
    }
    nc = bacc.Bacc("TRN2", target_bir_lowering=False, num_devices=1)
    aps = {n: nc.dram_tensor(f"in_{n}", v.shape, mybir.dt.from_np(v.dtype), kind="ExternalInput").ap()
           for n, v in arrays.items()}
    aps["out"] = nc.dram_tensor("out_rows", (G, P, B * D), F32, kind="ExternalOutput").ap()
    build(nc, aps)
    r = run_bass_kernel_spmd(nc, [{f"in_{n}": v for n, v in arrays.items()}], core_ids=[0])
    rows = r.results[0]["out_rows"]
    return flat(rows.reshape(G, P, B, D).transpose(0, 2, 1, 3)).reshape(N, D)
```

```python
from contextlib import ExitStack

import concourse.bass as bass
from concourse import mybir

N, D = 4096, 64
P = 128
JB = N // P
GC = 512
G = N // GC
B = GC // P
Q = G // 2
JP = JB // 2
NLOAD = 16
MAX_NEIGH = 100
STEP = 128
KEEP = 127 * STEP
CUT = KEEP - MAX_NEIGH * STEP
SCALE = 256.0
GATE = 4096.0
EPS = 1e-5
LAYERS = 5
EARLY = JB - 2 * B

ALU = mybir.AluOpType
ACT = mybir.ActivationFunctionType
AX = mybir.AxisListType.X
F32, F16, BF16 = mybir.dt.float32, mybir.dt.float16, mybir.dt.bfloat16
FP8, I16 = mybir.dt.float8e4, mybir.dt.int16



def build(nc, a):
    with ExitStack() as ctx:
        def sb(name, shape, dt=F32):
            return ctx.enter_context(nc.sbuf_tensor(name, shape, dt))

        def ps(name, shape):
            return ctx.enter_context(nc.psum_tensor(name, shape, F32))

        def sem(name):
            return ctx.enter_context(nc.semaphore(name))

        adjT = sb("adjT", [P, Q, JB, 2 * GC], FP8)
        x16 = sb("x16", [P, N], F16)
        m = sb("m", [P, 2, GC])
        m16 = sb("m16", [P, 2, GC], F16)
        xrow = sb("xrow", [P, JB, D])
        hrow = sb("hrow", [P, JB, D])
        S = [sb(f"S{i}", [P, JB, 2 * D], F16) for i in range(2)]
        wgt = sb("wgt", [P, 2, 2, GC], I16)
        yT = sb("yT", [P, 2, GC])
        rz0 = sb("rz", [P, B, 2 * D])
        rz = [rz0[:, :, :], wgt[:, 0, :, :].rearrange("p t c -> p (t c)").bitcast(F32).rearrange("p (b d) -> p b d", b=B)]
        nn = sb("nn", [P, B, D])
        t1 = sb("t1", [P, B, D])
        t2 = sb("t2", [P, B, D])
        ts = sb("ts", [P, B, D])
        z = sb("z", [P, B, D])
        zc = sb("zc", [P, B, D])
        sq = sb("sq", [P, B, D])
        stat = sb("stat", [P, 3, 2 * B])
        rstd = sb("rstd", [P, 2 * B])
        mhalf = sb("mhalf", [P, JB])
        ones = sb("ones", [P, GC], BF16)
        cutw = sb("cutw", [P, P], BF16)
        degsum = sb("degsum", [P, JB])
        deg1 = sb("deg1", [P, JB])
        rdeg = sb("rdeg", [P, JB])
        scaleb = sb("scaleb", [P, B])
        dinv = sb("dinv", [P, JB])
        dinvS = sb("dinvS", [P, JB])
        consts = sb("consts", [P, 3 * P])
        tri = sb("tri", [P, P], BF16)
        fix = sb("fix", [P, P], BF16)
        eye8 = sb("eye8", [P, P], FP8)
        w_y = sb("w_y", [P, 4 * D])
        raw = m[:, :, :].rearrange("p i c -> p (i c)")
        w_i, w_h = [raw[:, 6 * D * i:6 * D * (i + 1)].rearrange("p (l c) -> p l c", l=2) for i in range(2)]
        w_m = t1[:, :, :].rearrange("p b d -> p (b d)").rearrange("p (l c) -> p l c", l=2)
        wx16 = sb("wx16", [P, 2, 2, 3 * D], F16)
        wm16 = sb("wm16", [P, 2, 2, 3 * D], F16)
        gate1 = sb("gate1", [34, P], BF16)
        brow = rz0[0:2, :, :].rearrange("p b d -> p (b d)").rearrange("p (l c) -> p l c", l=2)
        b16 = sb("b16", [34, 2, 4 * D], F16)
        w_a16 = sb("w_a16", [P, 2, D], F16)
        bias0 = sb("bias0", [P, D])

        identity = consts[:, 2 * P:3 * P]

        Y = [ps(f"Y{c}", [P, GC]) for c in range(2)]
        both = ps("both", [P, 2, B, 4 * D])
        gates = [both[:, c, :, :] for c in range(2)]
        V = [both[:, 1, 2 * c:2 * c + 2, :].rearrange("p b d -> p (b d)") for c in range(2)]
        turn = [ps(f"turn{c}", [P, GC]) for c in range(2)]

        def rowsum(odd, half):
            return gates[odd][:, 2 * half, :].rearrange("p (b d) -> p b d", d=D)

        wide = [hrow[:, 2 * B * i:2 * B * (i + 1), :] for i in range(3)]
        picked = [rz0[:, :, :], hrow[:, 6 * B:8 * B, :].rearrange("p b d -> p (b d)").rearrange("p (b c) -> p b c", c=P)]

        load = [sem(f"load{i}") for i in range(NLOAD)]
        small_in = sem("small_in")
        gate_zero = sem("gate_zero")
        gate_in = sem("gate_in")
        gate_prod = sem("gate_prod")
        gate_const = sem("gate_const")
        x_in = [sem(f"x_in{g}") for g in range(G)]
        tri_in = sem("tri_in")
        consts_in = sem("consts_in")
        const_ready = sem("const_ready")
        bias_added = sem("bias_added")
        v_done = [sem(f"v_done{c}") for c in range(2)]
        w_ready = [sem(f"w_ready{c}") for c in range(2)]
        v_total = [sem(f"v_total{c}") for c in range(2)]
        deg_picked = [sem(f"deg_picked{c}") for c in range(2)]
        deg_in = sem("deg_in")
        deg_step = sem("deg_step")
        dinv_pow = sem("dinv_pow")
        dinv_ready = sem("dinv_ready")
        y_done = sem("y_done")
        y_half = sem("y_half")
        m_hi = sem("m_hi")
        m_ready = sem("m_ready")
        y0_out = [sem(f"y0_out{c}") for c in range(2)]
        y_out = sem("y_out")
        combined = sem("combined")
        sums_read = sem("sums_read")
        rz_ready = sem("rz_ready")
        n_in = sem("n_in")
        n_ready = sem("n_ready")
        chain = sem("chain")
        var_ready = sem("var_ready")
        rstd_ready = sem("rstd_ready")
        rows0_ready = sem("rows0_ready")
        rows_ready = sem("rows_ready")
        turned = sem("turned")
        xT_ready = sem("xT_ready")
        hi_ready = sem("hi_ready")
        t_ready = sem("t_ready")
        s_ready = sem("s_ready")
        stored = sem("stored")

        UNITS = [[(g * B, B) for g in range(G)] for _ in range(LAYERS)]
        UNITS[-1][-1:] = [(JB - B, B // 2), (JB - B // 2, B // 2)]

        def adj_tile(q, jb, c):
            return adjT[:, q, jb, c * GC:(c + 1) * GC]

        TURNS = {1: 0, 2: G, 4: 2 * G}
        SMALL = 16 * 9
        GATES = 16 * 20
        CONSTS = 11

        block = ctx.enter_context(nc.Block())

        @block.sync
        def _(sp):
            for g in range(G - 1, -1, -1):
                blk = slice(g * B, (g + 1) * B)
                sp.dma_start(xrow[:, blk, :], a["xrow"][:, blk, :]).then_inc(x_in[g], 16)
            sp.dma_start(bias0[:, :], a["bias"].to_broadcast([P, D])).then_inc(small_in, 16)
            for half in range(2):
                rows = slice(half * D, (half + 1) * D)
                sp.dma_start(w_y[rows, 0:D], a["L2W"]).then_inc(small_in, 16)
                sp.dma_start(w_y[rows, D:2 * D], a["L3WT"][D:2 * D, :]).then_inc(small_in, 16)
                sp.dma_start(w_y[rows, 2 * D:3 * D], a["L3WT"][0:D, :]).then_inc(small_in, 16)
                sp.dma_start(w_y[rows, 3 * D:4 * D], a["w0"]).then_inc(small_in, 16)
            for l in range(2):
                for half in range(2):
                    rows = slice(half * D, (half + 1) * D)
                    sp.dma_start(w_m[0:D, l, rows], a[f"W{l + 1}T"]).then_inc(gate_in, 16)
                    sp.dma_start(w_h[rows, l, 0:D], a[f"whh{l + 1}T"][:, 2 * D:3 * D]).then_inc(gate_in, 16)
                    sp.dma_start(w_h[rows, l, D:3 * D], a[f"whh{l + 1}T"][:, 0:2 * D]).then_inc(gate_in, 16)
                sp.dma_start(w_i[0:D, l, :], a[f"wih{l + 1}T"]).then_inc(gate_in, 16)
            sp.wait_ge(gate_zero, 2)
            for l in range(2):
                bih, bhh = a[f"bih{l + 1}"], a[f"bhh{l + 1}"]
                sp.dma_start(brow[0:1, l, D:4 * D], bih).then_inc(gate_in, 16)
                sp.dma_start(brow[1:2, l, 0:D], bhh[:, 2 * D:3 * D]).then_inc(gate_in, 16)
                sp.dma_start(brow[1:2, l, D:3 * D], bhh[:, 0:2 * D]).then_inc(gate_in, 16)
            for u, (b0, nb) in enumerate(UNITS[-1]):
                sp.wait_ge(rows_ready, 3 * G + u + 1)
                sp.dma_start(a["out"][:, b0:b0 + nb, :], xrow[:, b0:b0 + nb, :]).then_inc(stored, 16)
            sp.wait_ge(stored, 16 * len(UNITS[-1]))

        @block.gpsimd
        def _(pool):
            def root(n, blocks):
                pool.wait_ge(var_ready, n + 1)
                nc.gpsimd.tensor_tensor(rstd[:, 0:blocks], stat[:, 2, 0:blocks], mhalf[:, 0:blocks], ALU.pow)\
                    .then_inc(rstd_ready, 1)

            def split_rows(layer, g):
                blk = slice(g * B, (g + 1) * B)
                pool.wait_ge(rows_ready, (layer - 1) * G + g + 1)
                scale = dinvS[:, blk] if layer == 2 else scaleb[:, 0:B]
                pool.wait_ge(s_ready, (layer + 1) * G + g)
                rows = hrow if layer == 1 else xrow
                nc.gpsimd.tensor_tensor(ts[:, :, :], rows[:, blk, :], scale[:, :, None].to_broadcast([P, B, D]), ALU.mult)\
                    .then_inc(t_ready, 1)
                pool.wait_ge(t_ready, (layer - 1) * G + g + 1)
                pool.wait_ge(hi_ready, (layer - 1) * G + g + 1)
                s = S[(layer + 1) % 2][:, blk, :]
                nc.gpsimd.tensor_tensor(s[:, :, D:2 * D], ts[:, :, :], s[:, :, 0:D], ALU.subtract).then_inc(s_ready, 1)

            for q in range(Q):
                for n in range(JP):
                    i = q * JP + n
                    if i >= NLOAD:
                        pool.wait_ge(load[i % NLOAD], 16 * (i // NLOAD))
                    jp = JP - 1 - n
                    pool.dma_start(adjT[:, q, 2 * jp:2 * jp + 2, :], a["adjT"][q, jp]).then_inc(load[i % NLOAD], 16)
                    if i == 6:
                        pool.wait_ge(const_ready, CONSTS)
                        pool.wait_ge(small_in, SMALL)
                        pool.wait_ge(s_ready, G)
                        nc.gpsimd.tensor_tensor(xrow[:, :, :], xrow[:, :, :],
                                                bias0[:, None, :].to_broadcast([P, JB, D]), ALU.add).then_inc(bias_added, 1)
                    if q >= 2 and n == 13:
                        root(q - 2, 2 * B)
            root(Q - 2, 2 * B)
            root(Q - 1, 2 * B)
            pool.wait_ge(deg_step, 1)
            nc.gpsimd.tensor_tensor(dinv[:, :], deg1[:, :], mhalf[:, :], ALU.pow).then_inc(dinv_pow, 1)
            for g in range(G):
                split_rows(1, g)
            pool.wait_ge(dinv_ready, 2)
            for layer in (2, 3, 4):
                for g, (_, nb) in enumerate(UNITS[layer]):
                    root(Q + (layer - 2) * G + g, nb)
                    if layer < 4:
                        split_rows(layer, g)

        @block.scalar
        def _(act):
            act.dma_start(consts[:, 0:P], a["consts"][:, 0:P]).then_inc(tri_in, 16)
            act.dma_start(consts[:, P:3 * P], a["consts"][:, P:3 * P]).then_inc(consts_in, 16)

            def take_y(layer, g):
                e = layer * G + g
                act.wait_ge(y_done, e + 1)
                if layer == 0:
                    if g >= 2:
                        act.wait_ge(combined, g - 1)
                    nc.scalar.activation(yT[:, 0, :], Y[0][:, :], ACT.Copy).then_inc(y0_out[0], 1)
                    return
                act.wait_ge(combined, e - 1)
                nb = UNITS[layer][g][1]
                if layer in (1, 2):
                    nc.scalar.activation(yT[D:P, e % 2, :], Y[e % 2][0:D, :], ACT.Copy, scale=1.0 / SCALE).then_inc(y_half, 1)
                    act.wait_ge(y_out, e - G + 1)
                    nc.scalar.activation(m16[D:P, e % 2, :], m[D:P, e % 2, :], ACT.Copy).then_inc(m_hi, 1)
                else:
                    nc.scalar.activation(yT[:, e % 2, 0:nb * P], Y[e % 2][:, 0:nb * P], ACT.Copy).then_inc(y_out, 1)

            def take_xT(layer, g):
                act.wait_ge(turned, TURNS[layer] + g + 1)
                nc.scalar.activation(x16[:, g * GC:(g + 1) * GC], turn[g % 2][:, :], ACT.Copy).then_inc(xT_ready, 1)

            def hi_of_rows(layer, g):
                blk = slice(g * B, (g + 1) * B)
                hi = S[(layer + 1) % 2][:, blk, 0:D]
                if layer == 2:
                    act.wait_ge(t_ready, G + g + 1)
                    nc.scalar.activation(hi, ts[:, :, :], ACT.Copy).then_inc(hi_ready, 1)
                else:
                    act.wait_ge(rows_ready, (layer - 1) * G + g + 1)
                    rows = hrow if layer == 1 else xrow
                    nc.scalar.activation(hi, rows[:, blk, :], ACT.Copy, scale=SCALE).then_inc(hi_ready, 1)


            for q in range(Q):
                for t in range(JB):
                    for c in range(2):
                        act.wait_ge(v_done[c], q * JB + t + 1)
                        nc.scalar.activation(wgt[:, c, t % 2, :], V[c][:, :], ACT.Relu).then_inc(w_ready[c], 1)
                take_y(0, 2 * q)

            def gate(layer, g):
                e = layer * G + g
                act.wait_ge(combined, e + 1)
                if e > G + 1:
                    act.wait_ge(rows_ready, e - G - 1)
                nc.scalar.activation(rz[g % 2], gates[g % 2][:, :, D:3 * D], ACT.Sigmoid, scale=1.0 / GATE)\
                    .then_inc(rz_ready, 1)

            def new(layer, g):
                act.wait_ge(n_in, (layer - 1) * G + g + 1)
                nc.scalar.activation(nn[:, :, :], t2[:, :, :], ACT.Tanh).then_inc(n_ready, 1)

            for layer in range(1, LAYERS):
                units = len(UNITS[layer])
                if layer in TURNS:
                    take_xT(layer, 0)
                take_y(layer, 0)
                take_y(layer, 1)
                if layer in TURNS:
                    take_xT(layer, 1)
                for g in range(units):
                    if layer in (1, 2):
                        gate(layer, g)
                    if 1 <= g < G - 1 and layer in TURNS:
                        take_xT(layer, g + 1)
                    if layer in (1, 2):
                        if g >= 1:
                            hi_of_rows(layer, g - 1)
                        new(layer, g)
                    if 1 <= g < units - 1:
                        take_y(layer, g + 1)
                    if layer == 3:
                        hi_of_rows(layer, g)
                if layer in (1, 2):
                    hi_of_rows(layer, G - 1)

        @block.vector
        def _(dve):
            steps = [0]

            def did(ins):
                steps[0] += 1
                ins.then_inc(chain, 1)

            def after():
                dve.wait_ge(chain, steps[0])

            last = [0, 0]

            def both_halves(step, signal=None):
                for h in range(2):
                    if last[h] > 0:
                        dve.wait_ge(chain, last[h])
                    ins = step(h)
                    if h == 1 and signal is not None:
                        ins.then_inc(signal, 1)
                    else:
                        did(ins)
                        last[h] = steps[0]

            def halves(blocks):
                return [slice(h * blocks // 2, (h + 1) * blocks // 2) for h in range(2)]

            def norm(n, z, zc, sq, dst, ready, m_of=None):
                H = halves(z.shape[1])
                size = [P, z.shape[1] // 2, D]
                both_halves(lambda h: nc.vector.tensor_reduce(stat[:, 0, H[h]], z[:, H[h], :], AX, ALU.add))
                both_halves(lambda h: nc.vector.scalar_tensor_tensor(
                    out=zc[:, H[h], :], in0=stat[:, 0, H[h], None].to_broadcast(size), scalar=-1.0 / D,
                    in1=z[:, H[h], :], op0=ALU.mult, op1=ALU.add))
                if m_of is not None:
                    m_lo(m_of)
                both_halves(lambda h: nc.vector.tensor_tensor(sq[:, H[h], :], zc[:, H[h], :], zc[:, H[h], :], ALU.mult))
                both_halves(lambda h: nc.vector.tensor_reduce(stat[:, 1, H[h]], sq[:, H[h], :], AX, ALU.add))
                both_halves(lambda h: nc.vector.tensor_scalar(stat[:, 2, H[h]], stat[:, 1, H[h]], 1.0 / D, EPS,
                                                              ALU.mult, ALU.add), var_ready)
                dve.wait_ge(rstd_ready, n + 1)
                blocks = z.shape[1]
                nc.vector.tensor_tensor(dst, zc, rstd[:, 0:blocks, None].to_broadcast([P, blocks, D]), ALU.mult)\
                    .then_inc(ready, 1)

            def take_y(layer, g):
                e = layer * G + g
                if layer == 0:
                    dve.wait_ge(y_done, e + 1)
                    if g >= 2:
                        dve.wait_ge(combined, g - 1)
                    nc.vector.tensor_copy(yT[:, 1, :], Y[1][:, :]).then_inc(y0_out[1], 1)
                else:
                    dve.wait_ge(y_half, e - G + 1)
                    nc.vector.scalar_tensor_tensor(out=m[D:P, e % 2, :], in0=Y[e % 2][D:P, :], scalar=1.0 / SCALE,
                                                   in1=yT[D:P, e % 2, :], op0=ALU.mult, op1=ALU.add).then_inc(y_out, 1)

            def m_lo(e):
                dve.wait_ge(m_hi, e - G + 1)
                nc.vector.tensor_tensor(m16[0:D, e % 2, :], m[D:P, e % 2, :], m16[D:P, e % 2, :], ALU.subtract)\
                    .then_inc(m_ready, 1)

            def rows0(q):
                pair = xrow[:, 2 * q * B:(2 * q + 2) * B, :]
                if q == 0:
                    dve.wait_ge(bias_added, 1)
                dve.wait_ge(combined, 2 * q + 2)
                both_halves(lambda h: nc.vector.tensor_tensor(wide[0][:, h * B:(h + 1) * B, :], rowsum(0, h),
                                                              pair[:, h * B:(h + 1) * B, :], ALU.add))
                norm(q, wide[0], wide[1], wide[2], pair, rows0_ready)

            def pick_degree(q, c):
                dve.wait_ge(v_total[c], q + 1)
                if q >= 1:
                    dve.wait_ge(deg_in, 2 * q)
                nc.vector.tensor_tensor(picked[c], V[c][:, :].rearrange("p (b c) -> p b c", c=P),
                                        identity[:, None, :].to_broadcast([P, B, P]), ALU.mult)\
                    .then_inc(deg_picked[c], 1)

            def sum_degree(q):
                for c in range(2):
                    e = 2 * q + c
                    dve.wait_ge(deg_picked[c], q + 1)
                    nc.vector.tensor_reduce(degsum[:, e * B:(e + 1) * B], picked[c], AX, ALU.add).then_inc(deg_in, 1)

            def split_rows0(q):
                blk = slice(2 * q * B, (2 * q + 2) * B)
                dve.wait_ge(rows0_ready, q + 1)
                did(nc.vector.tensor_scalar(S[1][:, blk, 0:D], xrow[:, blk, :], SCALE, None, ALU.mult))
                after()
                nc.vector.scalar_tensor_tensor(out=S[1][:, blk, D:2 * D], in0=xrow[:, blk, :], scalar=SCALE,
                                               in1=S[1][:, blk, 0:D], op0=ALU.mult, op1=ALU.subtract).then_inc(s_ready, 2)

            nc.vector.memset(cutw[:, :], -float(CUT) / P).then_inc(const_ready, 1)
            nc.vector.memset(ones[:, :], 1.0).then_inc(const_ready, 1)
            nc.vector.memset(brow[:, :, :], 0.0).then_inc(gate_zero, 1)
            dve.wait_ge(tri_in, 16)
            nc.vector.tensor_copy(tri[:, :], consts[:, 0:P]).then_inc(const_ready, 1)
            dve.wait_ge(consts_in, 16)
            nc.vector.tensor_copy(fix[:, :], consts[:, P:2 * P]).then_inc(const_ready, 1)
            for g in range(G - 1, -1, -1):
                blk = slice(g * B, (g + 1) * B)
                dve.wait_ge(x_in[g], 16)
                did(nc.vector.tensor_scalar(S[0][:, blk, 0:D], xrow[:, blk, :], SCALE, None, ALU.mult))
                after()
                nc.vector.scalar_tensor_tensor(out=S[0][:, blk, D:2 * D], in0=xrow[:, blk, :], scalar=SCALE,
                                               in1=S[0][:, blk, 0:D], op0=ALU.mult, op1=ALU.subtract).then_inc(s_ready, 1)
                if g == G - 1:
                    nc.vector.memset(b16[:, :, :], 0.0).then_inc(gate_zero, 1)
                    nc.vector.memset(mhalf[:, :], -0.5).then_inc(const_ready, 1)
                    nc.vector.memset(scaleb[:, :], SCALE).then_inc(const_ready, 1)
                    nc.vector.memset(gate1[:, :], GATE).then_inc(const_ready, 1)
                    nc.vector.tensor_copy(eye8[:, :], consts[:, 2 * P:3 * P], saturate=False).then_inc(const_ready, 1)
            dve.wait_ge(small_in, SMALL)
            nc.vector.tensor_scalar(w_y[:, 0:2 * D], w_y[:, 0:2 * D], 1.0 / SCALE, None, ALU.mult).then_inc(const_ready, 1)
            did(nc.vector.tensor_scalar(w_a16[:, 0, :], w_y[:, 2 * D:3 * D], SCALE, None, ALU.mult))
            after()
            nc.vector.scalar_tensor_tensor(out=w_a16[:, 1, :], in0=w_y[:, 2 * D:3 * D], scalar=SCALE, in1=w_a16[:, 0, :],
                                           op0=ALU.mult, op1=ALU.subtract).then_inc(const_ready, 1)
            nc.vector.tensor_scalar(w_y[:, 3 * D:4 * D], w_y[:, 3 * D:4 * D], 2.0 ** (127 - MAX_NEIGH) / SCALE, None,
                                    ALU.mult).then_inc(const_ready, 1)
            dve.wait_ge(gate_in, GATES)
            did(nc.vector.tensor_scalar(wx16[:, :, 0, :], w_h, GATE / SCALE, None, ALU.mult))
            after()
            nc.vector.scalar_tensor_tensor(out=wx16[:, :, 1, :], in0=w_h, scalar=GATE / SCALE, in1=wx16[:, :, 0, :],
                                           op0=ALU.mult, op1=ALU.subtract).then_inc(gate_const, 1)
            nc.vector.tensor_copy(b16[0:2, :, :], brow[:, :, :]).then_inc(gate_const, 1)
            dve.wait_ge(gate_const, 2)
            nc.vector.tensor_tensor(b16[32:34, :, :], brow[:, :, :], b16[0:2, :, :], ALU.subtract).then_inc(gate_const, 1)
            dve.wait_ge(gate_const, 3)
            for q in range(Q):
                if q == Q - 1:
                    rows0(q - 1)
                    split_rows0(q - 1)
                pick_degree(q, 0)
                pick_degree(q, 1)
                take_y(0, 2 * q + 1)
                if q == 0:
                    dve.wait_ge(gate_prod, 2)
                    prod = gates[0][:, 0:4:2, 0:3 * D]
                    did(nc.vector.tensor_scalar(wm16[:, :, 0, :], prod, GATE, None, ALU.mult))
                    after()
                    nc.vector.scalar_tensor_tensor(out=wm16[:, :, 1, :], in0=prod, scalar=GATE, in1=wm16[:, :, 0, :],
                                                   op0=ALU.mult, op1=ALU.subtract).then_inc(gate_const, 1)
                if q < Q - 1:
                    sum_degree(q)
                if 1 <= q < Q - 1:
                    rows0(q - 1)
                    split_rows0(q - 1)
            rows0(Q - 1)
            split_rows0(Q - 1)

            def degrees():
                sum_degree(Q - 1)
                dve.wait_ge(deg_in, G)
                nc.vector.tensor_scalar(deg1[:, :], degsum[:, :], -1.0 / STEP, 1.0 - CUT / STEP, ALU.mult, ALU.add)\
                    .then_inc(deg_step, 1)
                dve.wait_ge(deg_step, 1)
                nc.vector.reciprocal(rdeg[:, :], deg1[:, :]).then_inc(dinv_ready, 1)

            def gated(layer, g, old, m_of=None):
                e = layer * G + g
                dve.wait_ge(rz_ready, e - G + 1)
                H = halves(B)
                gate_sums, rz_of = gates[g % 2], rz[g % 2]
                both_halves(lambda h: nc.vector.scalar_tensor_tensor(
                    out=t1[:, H[h], :], in0=gate_sums[:, H[h], 0:D], scalar=1.0 / GATE, in1=rz_of[:, H[h], 0:D],
                    op0=ALU.mult, op1=ALU.mult))
                both_halves(lambda h: nc.vector.scalar_tensor_tensor(
                    out=t2[:, H[h], :], in0=gate_sums[:, H[h], 3 * D:4 * D], scalar=1.0 / GATE, in1=t1[:, H[h], :],
                    op0=ALU.mult, op1=ALU.add), n_in)
                if m_of is not None:
                    take_y(layer, m_of - layer * G)
                    m_lo(m_of)
                dve.wait_ge(n_ready, e - G + 1)
                both_halves(lambda h: nc.vector.tensor_tensor(t1[:, H[h], :], old[:, H[h], :], nn[:, H[h], :], ALU.subtract))
                both_halves(lambda h: nc.vector.tensor_tensor(t2[:, H[h], :], t1[:, H[h], :], rz_of[:, H[h], D:2 * D], ALU.mult))
                both_halves(lambda h: nc.vector.tensor_tensor(z[:, H[h], :], t2[:, H[h], :], nn[:, H[h], :], ALU.add))

            degrees()
            for layer in range(1, LAYERS):
                if layer == 2:
                    dve.wait_ge(dinv_pow, 1)
                    nc.vector.tensor_scalar(dinvS[:, :], dinv[:, :], SCALE, None, ALU.mult).then_inc(dinv_ready, 1)
                    dve.wait_ge(dinv_ready, 2)
                for g, (b0, nb) in enumerate(UNITS[layer]):
                    e = layer * G + g
                    blk, H = slice(b0, b0 + nb), halves(nb)
                    if layer in (1, 2) and g == 0:
                        take_y(layer, 0)
                        if layer < 3:
                            m_lo(e)
                        take_y(layer, 1)
                        if layer < 3:
                            m_lo(e + 1)
                    if layer == 1:
                        gated(1, g, xrow[:, blk, :])
                        both_halves(lambda h: nc.vector.tensor_scalar(hrow[:, b0 + 2 * h:b0 + 2 * h + 2, :], z[:, H[h], :], 0.0,
                                                                      None, ALU.max), rows_ready)
                        if 1 <= g < G - 1:
                            take_y(1, g + 1)
                            m_lo(e + 1)
                        continue
                    if layer == 2:
                        soon = 1 <= g < G - 2
                        gated(2, g, hrow[:, blk, :], e + 1 if soon else None)
                        both_halves(lambda h: nc.vector.scalar_tensor_tensor(
                            out=z[:, H[h], :], in0=z[:, H[h], :], scalar=0.0, in1=xrow[:, blk, :][:, H[h], :],
                            op0=ALU.max, op1=ALU.add))
                        if g == G - 2:
                            take_y(2, g + 1)
                    if layer == 3:
                        dve.wait_ge(combined, e + 1)
                        both_halves(lambda h: nc.vector.tensor_tensor(
                            t2[:, H[h], :], rowsum(g % 2, 0)[:, H[h], :],
                            dinv[:, blk][:, H[h], None].to_broadcast([P, nb // 2, D]), ALU.mult), sums_read)
                        dve.wait_ge(sums_read, g + 1)
                        both_halves(lambda h: nc.vector.tensor_tensor(z[:, H[h], :], t2[:, H[h], :], xrow[:, blk, :][:, H[h], :],
                                                                      ALU.add))
                    if layer == 4:
                        dve.wait_ge(combined, e + 1)
                        both_halves(lambda h: nc.vector.tensor_tensor(
                            t2[:, H[h], :], rowsum(g % 2, 0)[:, H[h], :],
                            rdeg[:, blk][:, H[h], None].to_broadcast([P, nb // 2, D]), ALU.mult))
                        both_halves(lambda h: nc.vector.scalar_tensor_tensor(
                            out=t1[:, H[h], :], in0=rowsum(g % 2, 1)[:, H[h], :], scalar=SCALE ** -2, in1=t2[:, H[h], :],
                            op0=ALU.mult, op1=ALU.add), sums_read)
                        dve.wait_ge(sums_read, G + g + 1)
                        both_halves(lambda h: nc.vector.tensor_tensor(z[:, H[h], :], t1[:, H[h], :], xrow[:, blk, :][:, H[h], :],
                                                                      ALU.add))
                    norm(Q + (layer - 2) * G + g, z[:, 0:nb, :], zc[:, 0:nb, :], sq[:, 0:nb, :], xrow[:, blk, :], rows_ready,
                         e + 1 if layer == 2 and g == G - 2 else None)

        @block.tensor
        def _(pe):
            def transpose_features(layer, g):
                n = TURNS[layer] + g
                if n >= 2:
                    pe.wait_ge(xT_ready, n - 1)
                if g < 2:
                    pe.wait_ge(s_ready, layer * G + g + 1)
                for b in range(B):
                    mm = nc.tensor.matmul(turn[g % 2][:, b * P:(b + 1) * P], S[layer % 2][:, g * B + b, :], eye8[:, :],
                                          start=True, stop=True)
                mm.then_inc(turned, 1)

            def combine(layer, g):
                e = layer * G + g
                if layer == 0:
                    pe.wait_ge(y0_out[g % 2], g // 2 + 1)
                    if g >= 2:
                        pe.wait_ge(rows0_ready, g // 2)
                elif layer in (1, 2):
                    pe.wait_ge(m_ready, e - G + 1)
                else:
                    pe.wait_ge(y_out, e - G + 1)
                if layer in (1, 2, 4):
                    pe.wait_ge(xT_ready, TURNS[layer] + min(g + 1, G))
                if layer == 1 and g == 0:
                    pe.wait_ge(rows0_ready, Q)
                elif layer == 1 and g == 1:
                    pe.wait_ge(deg_picked[0], Q)
                    pe.wait_ge(deg_picked[1], Q)
                elif layer in (1, 2):
                    pe.wait_ge(n_in, e - G - 1)
                elif layer == 3 and g < 2:
                    pe.wait_ge(n_in, 2 * G - 1 + g)
                elif layer >= 3:
                    pe.wait_ge(sums_read, e - 3 * G - 1)
                b0, nb = UNITS[layer][g]
                for b in range(nb):
                    c0 = (b0 + b) * P
                    y = yT[:, g % 2, b * P:(b + 1) * P]
                    if layer == 0:
                        mm = nc.tensor.matmul(rowsum(0, g % 2)[:, b, :], y, w_y[:, 3 * D:4 * D], start=True, stop=True)
                    if layer in (1, 2):
                        l, to = layer - 1, gates[g % 2][:, b, :]
                        nc.tensor.matmul(to, gate1[:, :], b16[:, l, :], start=True, stop=True)
                        for part in range(2):
                            nc.tensor.matmul(to[:, 0:3 * D], x16[:, c0:c0 + P], wx16[:, l, part, :], start=False,
                                             stop=True, skip_group_check=True)
                        for part in range(2):
                            mm = nc.tensor.matmul(to[:, D:4 * D], m16[:, g % 2, b * P:(b + 1) * P], wm16[:, l, part, :],
                                                  start=False, stop=True, skip_group_check=True)
                    if layer == 3:
                        mm = nc.tensor.matmul(rowsum(g % 2, 0)[:, b, :], y, w_y[:, 0:D], start=True, stop=True)
                    if layer == 4:
                        nc.tensor.matmul(rowsum(g % 2, 0)[:, b, :], y, w_y[:, D:2 * D], start=True, stop=True)
                        own = rowsum(g % 2, 1)[:, b, :]
                        for part in range(2):
                            mm = nc.tensor.matmul(own, x16[:, c0:c0 + P], w_a16[:, part, :], start=(part == 0), stop=(part == 1))
                mm.then_inc(combined, 1)

            def weigh(q, t, c):
                if t == 0 and q >= 1:
                    pe.wait_ge(y0_out[c], q)
                jb = JB - 1 - t
                if q == 0 and t % B == 0:
                    pe.wait_ge(s_ready, t // B + 1)
                mm = nc.tensor.matmul(Y[c][:, :], S[0][:, jb, :], wgt[:, c, t % 2, :].bitcast(BF16),
                                      start=(t == 0), stop=(t == JB - 1), skip_group_check=True)
                if t == JB - 1:
                    mm.then_inc(y_done, 1)

            pe.wait_ge(const_ready, 2)
            for _ in range(6):
                nc.tensor.matmul(V[0][:, :], cutw[:, :], ones[:, :], start=True, stop=True)
            pe.wait_ge(const_ready, 3)
            for q in range(Q):
                for t in range(JB):
                    jb = JB - 1 - t
                    if t % 2 == 0:
                        i = q * JP + t // 2
                        pe.wait_ge(load[i % NLOAD], 16 * (i // NLOAD + 1))
                    for c in range(2):
                        if t == 0:
                            if q >= 1:
                                pe.wait_ge(deg_picked[c], q)
                            nc.tensor.matmul(V[c][:, :], cutw[:, :], ones[:, :], start=True, stop=False,
                                             skip_group_check=True)
                        else:
                            if q == 0 and t == 1:
                                pe.wait_ge(const_ready, 4)
                            pe.wait_ge(w_ready[c], q * JB + t)
                            nc.tensor.matmul(V[c][:, :], fix[:, :], adj_tile(q, jb + 1, c), start=False, stop=False,
                                             skip_group_check=True)
                        nc.tensor.matmul(V[c][:, :], tri[:, :], adj_tile(q, jb, c), start=False, stop=False,
                                         skip_group_check=True).then_inc(v_done[c], 1)
                        if t >= 1:
                            weigh(q, t - 1, c)
                    if q == Q - 1 and t == 6:
                        combine(0, 2 * q - 2)
                        combine(0, 2 * q - 1)
                if q == 0:
                    pe.wait_ge(gate_in, GATES)
                if q == 1:
                    pe.wait_ge(const_ready, CONSTS)
                    pe.wait_ge(gate_const, 4)
                for c in range(2):
                    if q == 0:
                        mm = nc.tensor.matmul(gates[0][:, 2 * c, 0:3 * D], w_m[0:D, c, :], w_i[0:D, c, :], start=True, stop=True)
                        mm.then_inc(gate_prod, 1)
                    elif q < Q - 1:
                        combine(0, 2 * q - 2 + c)
                    pe.wait_ge(w_ready[c], (q + 1) * JB)
                    nc.tensor.matmul(V[c][:, :], fix[:, :], adj_tile(q, 0, c), start=False, stop=True,
                                     skip_group_check=True).then_inc(v_total[c], 1)
                    weigh(q, JB - 1, c)

            def product(layer, g, first, last):
                if first == last:
                    return
                if first == 0:
                    if layer == 1 and g < 2:
                        pe.wait_ge(y0_out[g], Q)
                    else:
                        pe.wait_ge(y_out, (layer - 1) * G + g - 1)
                b0, nb = UNITS[layer][g]
                q, c0 = b0 // (2 * B), b0 % (2 * B) * P
                cols = adjT[:, q, :, c0:c0 + nb * P]
                for jb in range(first, last):
                    if g < 2 and jb % B == 0:
                        pe.wait_ge(s_ready, layer * G + jb // B + 1)
                    mm = nc.tensor.matmul(Y[g % 2][:, 0:nb * P], S[layer % 2][:, jb, :], cols[:, jb, :],
                                          start=(jb == 0), stop=(jb == JB - 1), skip_group_check=True)
                if last == JB:
                    if layer == 3:
                        for b in range(B):
                            mm = nc.tensor.matmul(Y[g % 2][:, b * P:(b + 1) * P], S[1][:, g * B + b, :], eye8[:, :],
                                                  start=False, stop=True, skip_group_check=True)
                    mm.then_inc(y_done, 1)

            def first_two(layer, a, b):
                at = 0
                for g, lo, hi in ((0, 0, EARLY), (1, 0, EARLY), (0, EARLY, JB - B), (1, EARLY, EARLY + 2),
                                  (0, JB - B, JB), (1, EARLY + 2, JB)):
                    x, y = max(a, at), min(b, at + hi - lo)
                    if x < y:
                        product(layer, g, lo + x - at, lo + y - at)
                    at += hi - lo

            for layer in range(1, LAYERS):
                c, t = {1: (7, 48), 2: (14, 50), 3: (19, 50), 4: (5, 50)}[layer]
                first_two(layer, 0, c)
                if layer == 1:
                    combine(0, G - 2)
                combine(layer - 1, G - 1)
                first_two(layer, c, t)
                if layer in TURNS:
                    transpose_features(layer, 0)
                first_two(layer, t, 64)
                if layer in TURNS:
                    transpose_features(layer, 1)
                for g in range(2, len(UNITS[layer])):
                    first = g == 2
                    if first:
                        early = {1: 10, 2: 10, 3: 4, 4: 4}[layer]
                        product(layer, g, 0, early)
                        combine(layer, 0)
                    c, t = {1: (15, 15), 2: (16, 16), 3: (6, 14), 4: (6, 14)}[layer]
                    if layer == 2 and g < 6:
                        c = {2: 16, 3: 18, 4: 20, 5: 19}[g]
                    elif first:
                        c = 18 if layer == 1 else 12
                    elif g >= G - 1 and layer == 4:
                        c = 10
                    t = max(c, t)
                    product(layer, g, early if first else 0, c)
                    combine(layer, g - 1)
                    product(layer, g, c, t)
                    if layer in TURNS and g < G:
                        transpose_features(layer, g)
                    product(layer, g, t, JB)
            combine(LAYERS - 1, len(UNITS[-1]) - 1)


def kernel(x, adj, L0_gnn_weight, L0_gnn_bias, L1_gnn_W1, L1_gnn_wih1, L1_gnn_whh1, L1_gnn_bih1, L1_gnn_bhh1,
           L1_gnn_W2, L1_gnn_wih2, L1_gnn_whh2, L1_gnn_bih2, L1_gnn_bhh2, L2_gnn_W, L3_gnn_W):
    import numpy as np
    import concourse.bacc as bacc
    from concourse.bass_utils import run_bass_kernel_spmd

    def flat(v):
        return np.ascontiguousarray(v)

    x, adj = np.asarray(x), np.asarray(adj)
    behind = np.tril(np.ones((P, P), np.float32), -1)
    eye = np.eye(P, dtype=np.float32)
    tri = KEEP * eye - STEP * behind
    arrays = {
        "adjT": flat(adj.reshape(Q, 2 * GC, JP, 2, P).transpose(0, 2, 4, 3, 1)).reshape(Q, JP, P, 4 * GC),
        "xrow": flat(x.reshape(JB, P, D).transpose(1, 0, 2)),
        "consts": flat(np.concatenate([tri, -STEP - tri, eye], axis=1)),
        "w0": flat(L0_gnn_weight), "bias": flat(np.asarray(L0_gnn_bias).reshape(1, D)),
        "W1T": flat(np.asarray(L1_gnn_W1).T), "W2T": flat(np.asarray(L1_gnn_W2).T),
        "wih1T": flat(np.asarray(L1_gnn_wih1).T), "wih2T": flat(np.asarray(L1_gnn_wih2).T),
        "whh1T": flat(np.asarray(L1_gnn_whh1).T), "whh2T": flat(np.asarray(L1_gnn_whh2).T),
        "bih1": flat(np.asarray(L1_gnn_bih1).reshape(1, 3 * D)), "bhh1": flat(np.asarray(L1_gnn_bhh1).reshape(1, 3 * D)),
        "bih2": flat(np.asarray(L1_gnn_bih2).reshape(1, 3 * D)), "bhh2": flat(np.asarray(L1_gnn_bhh2).reshape(1, 3 * D)),
        "L2W": flat(L2_gnn_W), "L3WT": flat(np.asarray(L3_gnn_W).T),
    }
    nc = bacc.Bacc("TRN2", target_bir_lowering=False, num_devices=1)
    aps = {n: nc.dram_tensor(f"in_{n}", v.shape, mybir.dt.from_np(v.dtype), kind="ExternalInput").ap()
           for n, v in arrays.items()}
    aps["out"] = nc.dram_tensor("out_rows", (P, JB, D), F32, kind="ExternalOutput").ap()
    build(nc, aps)
    r = run_bass_kernel_spmd(nc, [{f"in_{n}": v for n, v in arrays.items()}], core_ids=[0])
    rows = r.results[0]["out_rows"]
    return flat(rows.reshape(P, JB, D).transpose(1, 0, 2)).reshape(N, D)
```
